# Optimizing a Trainium2 kernel written in Bass

```python
import numpy as np
import jax
import jax.numpy as jnp

def _softmax(x, axis=-1):
    return jax.nn.softmax(x, axis=axis)

def _gelu(x):
    return jax.nn.gelu(x, approximate=True)

def _silu(x):
    return jax.nn.silu(x)

def _sigmoid(x):
    return jax.nn.sigmoid(x)

def _layernorm(x, axis=-1, eps=1e-05):
    m = jnp.mean(x, axis=axis, keepdims=True)
    v = jnp.var(x, axis=axis, keepdims=True)
    return (x - m) / jnp.sqrt(v + eps)

def _scatter_add(tgt, idx, src, axis=0):
    return tgt.at[idx].add(src)

def _segment_sum(src, seg, n):
    return jax.ops.segment_sum(src, seg, n)
kernel_name = 'mk_seq_postln_d1_jaxref_r8_5dfa99'

def setup_inputs(seed: int=0):
    np.random.seed(seed)
    _w = jnp.asarray

    def _L0_attn_setup():
        import jax, jax.numpy as jnp
        import numpy as np
        D_MODEL = 128
        N_HEADS = 16
        TOP_FACTOR = 5
        key = jax.random.key(seed)
        ks = jax.random.split(key, 9)
        B, L, D = (2, 512, D_MODEL)
        s = 0.02
        return {'x': jax.random.normal(ks[0], (B, L, D), dtype=jnp.float32), 'Wq': jax.random.normal(ks[1], (D, D), dtype=jnp.float32) * s, 'bq': jnp.zeros((D,), dtype=jnp.float32), 'Wk': jax.random.normal(ks[2], (D, D), dtype=jnp.float32) * s, 'bk': jnp.zeros((D,), dtype=jnp.float32), 'Wv': jax.random.normal(ks[3], (D, D), dtype=jnp.float32) * s, 'bv': jnp.zeros((D,), dtype=jnp.float32), 'Wo': jax.random.normal(ks[4], (D, D), dtype=jnp.float32) * s, 'bo': jnp.zeros((D,), dtype=jnp.float32)}
    _L0_attn_in = _L0_attn_setup()

    def _L0_ffn_setup():
        import jax, jax.numpy as jnp
        import numpy as np
        B, T, D, E, H = (4, 256, 128, 4, 8)
        EPS = 1e-05

        def _uniform(k, shape, bound):
            return jax.random.uniform(k, shape, jnp.float32, -bound, bound)

        def _layernorm(x, w, b):
            mu = jnp.mean(x, axis=-1, keepdims=True)
            var = jnp.mean(jnp.square(x - mu), axis=-1, keepdims=True)
            return (x - mu) * jax.lax.rsqrt(var + EPS) * w + b
        key = jax.random.key(seed)
        ks = jax.random.split(key, 12)
        wb = np.sqrt(6.0 / D) / np.sqrt(6.0)
        wb = 1.0 / np.sqrt(D)
        return {'x': jax.random.normal(ks[0], (B, T, D), jnp.float32), 'router_prob': jax.random.uniform(ks[1], (B, T, E), jnp.float32), 'norm_w': jnp.ones((D,), jnp.float32), 'norm_b': jnp.zeros((D,), jnp.float32), 'q_w': _uniform(ks[2], (D, D), wb), 'q_b': _uniform(ks[3], (D,), wb), 'k_w': _uniform(ks[4], (D, D), wb), 'k_b': _uniform(ks[5], (D,), wb), 'v_w': _uniform(ks[6], (D, D), wb), 'v_b': _uniform(ks[7], (D,), wb), 'o_w': _uniform(ks[8], (D, D), wb), 'o_b': _uniform(ks[9], (D,), wb)}
    _L0_ffn_in = _L0_ffn_setup()
    _d = {'L0_attn_x': _L0_attn_in['x'], 'L0_attn_Wq': _L0_attn_in['Wq'], 'L0_attn_bq': _L0_attn_in['bq'], 'L0_attn_Wk': _L0_attn_in['Wk'], 'L0_attn_bk': _L0_attn_in['bk'], 'L0_attn_Wv': _L0_attn_in['Wv'], 'L0_attn_bv': _L0_attn_in['bv'], 'L0_attn_Wo': _L0_attn_in['Wo'], 'L0_attn_bo': _L0_attn_in['bo'], 'L0_ffn_router_prob': _L0_ffn_in['router_prob'], 'L0_ffn_norm_w': _L0_ffn_in['norm_w'], 'L0_ffn_norm_b': _L0_ffn_in['norm_b'], 'L0_ffn_q_w': _L0_ffn_in['q_w'], 'L0_ffn_q_b': _L0_ffn_in['q_b'], 'L0_ffn_k_w': _L0_ffn_in['k_w'], 'L0_ffn_k_b': _L0_ffn_in['k_b'], 'L0_ffn_v_w': _L0_ffn_in['v_w'], 'L0_ffn_v_b': _L0_ffn_in['v_b'], 'L0_ffn_o_w': _L0_ffn_in['o_w'], 'L0_ffn_o_b': _L0_ffn_in['o_b']}
    _x0 = _d['L0_attn_x']
    _d['L0_attn_x'] = jax.random.normal(jax.random.fold_in(jax.random.key(seed), 1), (4, 1024, 128), dtype=_x0.dtype)
    del _x0
    return _d

def reference(L0_attn_x, L0_attn_Wq, L0_attn_bq, L0_attn_Wk, L0_attn_bk, L0_attn_Wv, L0_attn_bv, L0_attn_Wo, L0_attn_bo, L0_ffn_router_prob, L0_ffn_norm_w, L0_ffn_norm_b, L0_ffn_q_w, L0_ffn_q_b, L0_ffn_k_w, L0_ffn_k_b, L0_ffn_v_w, L0_ffn_v_b, L0_ffn_o_w, L0_ffn_o_b):

    def _L0_attn_ref(x, Wq, bq, Wk, bk, Wv, bv, Wo, bo):
        import jax, jax.numpy as jnp
        import numpy as np
        D_MODEL = 128
        N_HEADS = 16
        TOP_FACTOR = 5
        B, L, D = x.shape
        H = N_HEADS
        hd = D // H
        BH = B * H
        top_u = max(1, L // TOP_FACTOR)

        def proj(W, b):
            y = x @ W.T + b
            return y.reshape(B, L, H, hd).transpose(0, 2, 1, 3).reshape(BH, L, hd)
        Q = proj(Wq, bq)
        K = proj(Wk, bk)
        V = proj(Wv, bv)
        query_norms = jnp.linalg.norm(Q, axis=2)
        _, top_idx = jax.lax.top_k(query_norms, top_u)
        Q_sel = jnp.take_along_axis(Q, top_idx[:, :, None], axis=1)
        scale = 1.0 / hd ** 0.5
        scores = jnp.einsum('bud,bld->bul', Q_sel, K) * scale
        attn = jax.nn.softmax(scores, axis=-1)
        out_sel = jnp.einsum('bul,bld->bud', attn, V)
        out_full = jnp.zeros((BH, L, hd), dtype=x.dtype)
        out_full = out_full.at[jnp.arange(BH)[:, None], top_idx].set(out_sel)
        out = out_full.reshape(B, H, L, hd).transpose(0, 2, 1, 3).reshape(B, L, D)
        return out @ Wo.T + bo

    def _L0_ffn_ref(x, router_prob, norm_w, norm_b, q_w, q_b, k_w, k_b, v_w, v_b, o_w, o_b):
        import jax, jax.numpy as jnp
        import numpy as np
        B, T, D, E, H = (4, 256, 128, 4, 8)
        EPS = 1e-05

        def _uniform(k, shape, bound):
            return jax.random.uniform(k, shape, jnp.float32, -bound, bound)

        def _layernorm(x, w, b):
            mu = jnp.mean(x, axis=-1, keepdims=True)
            var = jnp.mean(jnp.square(x - mu), axis=-1, keepdims=True)
            return (x - mu) * jax.lax.rsqrt(var + EPS) * w + b
        e_cnt = router_prob.shape[2]
        b, t, d = x.shape
        n = t // e_cnt
        h = H
        scale = d ** (-0.5)
        qs, ks_, vs = ([], [], [])
        for e in range(e_cnt):
            xe = x[:, e * n:(e + 1) * n, :]
            xn = _layernorm(xe, norm_w, norm_b)
            m = d // 2 ** e
            xm = xn[..., :m]
            qs.append(jnp.einsum('bnm,dm->bnd', xm, q_w[:, :m]) + q_b)
            ks_.append(jnp.einsum('bnm,dm->bnd', xm, k_w[:, :m]) + k_b)
            vs.append(jnp.einsum('bnm,dm->bnd', xm, v_w[:, :m]) + v_b)
        q = jnp.concatenate(qs, axis=1)
        k = jnp.concatenate(ks_, axis=1)
        v = jnp.concatenate(vs, axis=1)
        dh = d // h
        q = q.reshape(b, t, h, dh).transpose(0, 2, 1, 3)
        k = k.reshape(b, t, h, dh).transpose(0, 2, 1, 3)
        v = v.reshape(b, t, h, dh).transpose(0, 2, 1, 3)
        attn = jnp.einsum('bhqd,bhkd->bhqk', q, k) * scale
        attn = jax.nn.softmax(attn, axis=-1)
        attn_out = jnp.einsum('bhqk,bhkd->bhqd', attn, v)
        attn_out = attn_out.transpose(0, 2, 1, 3).reshape(b, t, d)
        outs = []
        for e in range(e_cnt):
            sl = slice(e * n, (e + 1) * n)
            m = d // 2 ** e
            xm = attn_out[:, sl, :m]
            out = jnp.einsum('bnm,om->bno', xm, o_w[:m, :m]) + o_b[:m]
            pad = d - m
            if pad:
                out = jnp.pad(out, ((0, 0), (0, 0), (0, pad)))
            outs.append(out + x[:, sl, :])
        return jnp.concatenate(outs, axis=1)
    x = L0_attn_x
    x = _layernorm(x + _L0_attn_ref(x, L0_attn_Wq, L0_attn_bq, L0_attn_Wk, L0_attn_bk, L0_attn_Wv, L0_attn_bv, L0_attn_Wo, L0_attn_bo), axis=-1)
    x = _layernorm(x + _L0_ffn_ref(x, L0_ffn_router_prob, L0_ffn_norm_w, L0_ffn_norm_b, L0_ffn_q_w, L0_ffn_q_b, L0_ffn_k_w, L0_ffn_k_b, L0_ffn_v_w, L0_ffn_v_b, L0_ffn_o_w, L0_ffn_o_b), axis=-1)
    return x

_drawn_inputs = setup_inputs


def setup_inputs(seed=0):
    import zlib

    import numpy as np

    out = dict(_drawn_inputs(seed))
    spreads = {'L0_attn_bq': (0.0, 0.8),
     'L0_attn_bk': (0.0, 2.0),
     'L0_attn_bv': (0.0, 0.8),
     'L0_attn_bo': (0.0, 0.1),
     'L0_ffn_norm_w': (1.0, 0.6),
     'L0_ffn_norm_b': (0.0, 0.8)}
    factors = {'L0_attn_Wq': 6.739,
     'L0_attn_Wk': 8.0,
     'L0_attn_Wv': 8.0,
     'L0_attn_Wo': 6.0,
     'L0_ffn_q_w': 8.0,
     'L0_ffn_q_b': 8.0,
     'L0_ffn_k_w': 8.0,
     'L0_ffn_k_b': 64.0,
     'L0_ffn_v_w': 6.121,
     'L0_ffn_v_b': 6.885,
     'L0_ffn_o_w': 4.976,
     'L0_ffn_o_b': 9.993}
    for name, (base, spread) in spreads.items():
        noise = np.random.default_rng([zlib.crc32(name.encode()), seed]).standard_normal(out[name].shape)
        drawn = base * np.exp(spread * noise) if base else spread * noise
        out[name] = jnp.asarray(drawn.astype(out[name].dtype))
    for name, factor in factors.items():
        out[name] = (out[name] * factor).astype(out[name].dtype)
    return out
```

```python
from contextlib import ExitStack

import concourse.bass as bass
from concourse import mybir

ALU = mybir.AluOpType
ACT = mybir.ActivationFunctionType
AX_X = mybir.AxisListType.X
F32 = mybir.dt.float32
BF16 = mybir.dt.bfloat16
I32 = mybir.dt.int32

P = 128
B = 4
T = 1024
D = 128
TT = T // P
EPS = 1e-5

H1 = 16
HD1 = D // H1
TOP = T // 5
HALF = TOP // 2
PAIRS = H1 // 2

H2 = 8
HD2 = D // H2
SEG = 4

K_SLOTS = (0, 1, 0, 1, 2, 0)
Q_SLOTS = (0, 0, 1, 1, 0, 2)
SLOTS = len(K_SLOTS)
ROWS = 16 * SLOTS
GUARD = 2
KR = ROWS + GUARD
VW = 32

QTS = 4
RING = 4
AHEAD = 2

SHIFTS = tuple(range(28, 0, -3)) + (0,)
ROUNDS = len(SHIFTS)


class Layer:

    def __init__(self, index):
        self.one = index == 1
        self.units = PAIRS if self.one else 2 * H2
        self.u0 = 0 if self.one else PAIRS
        self.qw = HALF if self.one else P
        self.nq = QTS * self.qw
        self.scale = HD1 ** -0.5 if self.one else D ** -0.5
        self.hd = HD1 if self.one else HD2

    def slot(self, u):
        return (u if self.one else u // 2) % RING

    def q0(self, u):
        return 0 if self.one else u % 2 * self.nq


L1, L2 = Layer(1), Layer(2)
UB = L1.units + L2.units


def small_bank_plan():
    plan = [("round", r) for r in range(ROUNDS)] + [("position", 0)]
    plan += [("gather", 1, 0), ("gather", 1, 1), ("guard", 1, 0), ("guard", 1, 1)]
    for L, n in ((L1, 1), (L2, 2)):
        if n == 2:
            plan += [("guard", 2, 0), ("guard", 2, 1)]
        for u in range(L.units + 1):
            if n == 1 and u + AHEAD < L.units:
                plan.append(("gather", n, u + AHEAD))
            if u > 0:
                plan.append(("turn", n, u - 1))
                if n == 1:
                    plan.append(("scatter", n, u - 1))
            if u + AHEAD < L.units:
                plan.append(("guard", n, u + AHEAD))
    return {key: i for i, key in enumerate(plan)}


X_PLAN = small_bank_plan()
X_USES = len(X_PLAN)


def build(nc, t_in, out):
    ctx = ExitStack()
    with ctx:
        def sb(name, shape, dt=F32):
            return ctx.enter_context(nc.sbuf_tensor(name, shape, dt))

        def ps(name, shape, dt=F32):
            return ctx.enter_context(nc.psum_tensor(name, shape, dt))

        def sem(name):
            return ctx.enter_context(nc.semaphore(name))

        k_dram = nc.dram_tensor("k_parts", (D, SLOTS, T), BF16, kind="Internal").ap()
        q_dram = nc.dram_tensor("q_parts", (D, SLOTS, T), BF16, kind="Internal").ap()
        pos_dram = nc.dram_tensor("positions", (H1, T), BF16, kind="Internal").ap()

        wqT, wkT, wvT, woT = (sb(n, [P, D]) for n in ("wqT", "wkT", "wvT", "woT"))
        q2w, k2w, v2w = (sb(n, [P, D]) for n in ("q2w", "k2w", "v2w"))
        o2w = sb("o2w", [P, SEG, D])
        rows = sb("rows", [1, 4, D])
        o2b = sb("o2b", [1, SEG, D])
        cols = sb("cols", [P, 5])
        ones_row = sb("ones_row", [1, P])
        ident = sb("ident", [P, P])
        ident_b = sb("ident_b", [P, P], BF16)
        same_head = sb("same_head", [P, P], BF16)
        iota_u = sb("iota_u", [P, TOP], BF16)
        iota_i = sb("iota_i", [P, TOP], I32)
        iota_p = sb("iota_p", [P, 2])
        iota_pi = sb("iota_pi", [P, 2], I32)
        lane = sb("lane", [P, 2], I32)
        digit = sb("digit", [P, ROUNDS], I32)
        ones_t = sb("ones_t", [P, T])
        eps_c = sb("eps_c", [P, 1])

        xT = sb("xT", [P, T])
        x_tok = sb("x_tok", [P, TT, D])
        q32 = sb("q32", [P, T])
        k32 = sb("k32", [P, T])
        n2 = sb("n2", [P, TT * H1])
        n2rep = sb("n2rep", [P, TT, H1, 8])
        norms = sb("norms", [P, T])
        cmp = sb("cmp", [P, T])
        cum = sb("cum", [P, T])
        pos_row = sb("pos_row", [P, T], BF16)
        pos_col = sb("pos_col", [P, TT, H1])
        found = sb("found", [P, 3], I32)
        count = sb("count", [P, 2])
        count_b = sb("count_b", [P, 1], BF16)
        rest = sb("rest", [P, T])
        k_part = [sb(f"k_part{i}", [P, T], BF16) for i in range(3)]
        q_part = [sb(f"q_part{i}", [P, T], BF16) for i in range(3)]
        q_slots = sb("q_slots", [P, TT, H1, ROWS], BF16)
        v1_all = sb("v1_all", [P, PAIRS, TT, 2, VW])
        v2_all = sb("v2_all", [P, H2, TT, VW])
        att = sb("att", [P, TT, D])
        x1 = sb("x1", [P, TT, D])
        zt = sb("zt", [P, TT, D])
        xh = sb("xh", [P, TT, D])
        tr = sb("tr", [P, T])
        stats = sb("stats", [P, TT, 6])
        mv = sb("mv", [P, TT, 2])
        std = sb("std", [P, TT])
        rstd = sb("rstd", [P, TT])

        keys = sb("keys", [KR, RING, T], BF16)
        queries = sb("queries", [KR, RING, T], BF16)
        values = sb("values", [P, RING, TT * 2 * VW])
        sel = sb("sel", [P, 2, 2, TT, TOP], BF16)
        sel_t = sb("sel_t", [HALF, 2, 2, 2, T], BF16)
        pos_b = sb("pos_b", [HALF, 2, 2, T], BF16)
        probs = sb("probs", [P, RING, 512])
        mx = sb("mx", [P, QTS])
        mx_rest = sb("mx_rest", [P, QTS])
        g_part = sb("g_part", [P, 2, GUARD, QTS], BF16)
        g_row = sb("g_row", [GUARD * QTS, RING, P], BF16)
        pv_sb = sb("pv_sb", [P, 2, P])
        den = sb("den", [P, QTS])
        o_sel = sb("o_sel", [HALF, QTS, HD1])
        o_rest = sb("o_rest", [HALF, QTS, HD1])
        o_part = sb("o_part", [HALF, 2, QTS, 3, HD1], BF16)

        mbank = [ps(f"mbank{i}", [P, 1024]) for i in range(2)]
        sbank = [ps(f"sbank{i}", [P, 512]) for i in range(2)]
        vbank = ps("vbank", [P, 512])
        xbank = ps("xbank", [P, 512])
        xbank_b = xbank[:, :].bitcast(BF16)

        w_in, w_zero = sem("weights_loaded"), sem("weights_zeroed")
        c_pool, c_vec, c_rdy = sem("constants_pool"), sem("constants_vector"), sem("constants_ready")
        xT_in, x_in = sem("xT_loaded"), sem("x_tokens_loaded")
        q_mm, k_mm, v_mm = sem("q_product"), sem("k_product"), sem("v_product")
        q_ev, k_ev, v_ev = sem("q_copied"), sem("k_copied"), sem("v_copied")
        n2_rdy, nt_mm, nt_ev = sem("norms_ready"), sem("norms_turned"), sem("norms_copied")
        cnt_rdy = sem("count_ready")
        pos_rdy, pos_out = sem("positions_ready"), sem("positions_stored")
        qp_rdy, kp_rdy, qs_rdy = sem("q_parts_ready"), sem("k_parts_ready"), sem("q_slots_ready")
        p_out = sem("parts_stored")
        p_step, v_step = sem("pool_step"), sem("vector_step")
        kv_in = [sem(f"unit_loaded{i}") for i in range(RING)]
        pb_in = [sem(f"position_rows_loaded{i}") for i in range(2)]
        sel_rdy, selt_v, selt_p = sem("sel_ready"), sem("sel_t_vector"), sem("sel_t_pool")
        max_mm, max_red = sem("max_scores"), sem("max_reduced")
        gp_rdy, on_rdy = sem("guard_parts"), sem("outputs_normed")
        x_mm, x_read = sem("small_bank_written"), sem("small_bank_read")
        guard_in = [sem(f"guard_rows_loaded{i}") for i in range(RING)]
        score_mm, exp_done, pv_mm, pv_ev = sem("scores"), sem("exponentials"), sem("values_added"), sem("values_copied")
        tr_mm, tr_ev, z_mm = sem("turned"), sem("turned_copied"), sem("output_product")
        sd_rdy, rt_rdy, n_rdy = sem("variance_ready"), sem("deviation_ready"), sem("normed")
        y_out = sem("output_stored")
        p_hold, v_hold, s_hold = sem("pool_hold"), sem("vector_hold"), sem("dma_hold")

        def unit_no(b, L, u):
            return b * UB + (L.u0 + u)

        def tile_no(b, L, u, kt):
            return b * (UB * TT) + ((L.u0 + u) * TT + kt)

        def qt_no(b, L, u, q):
            return b * (UB * QTS) + ((L.u0 + u) * QTS + q)

        def x_no(b, *key):
            return b * X_USES + X_PLAN[key]

        def kv_count(b, L, u):
            own = 2 * (u // RING + 1) if L.one else 4 + 3 * (u // 2 // RING + 1)
            return b * 160 + 16 * own

        def guard_count(b, L, u):
            return b * (32 * UB // RING) + 32 * ((L.u0 + u) // RING + 1)

        block = ctx.enter_context(nc.Block())

        @block.sync
        def _(sp):
            for dst, name in ((wqT, "WqT"), (wkT, "WkT"), (wvT, "WvT"), (woT, "WoT"),
                              (q2w, "q_wT"), (k2w, "k_wT"), (v2w, "v_wT")):
                sp.dma_start(dst[:, :], t_in[name]).then_inc(w_in, 16)
            for i, name in enumerate(("bq", "bv", "bo", "v_b")):
                sp.dma_start(rows[:, i, :], t_in[name]).then_inc(w_in, 16)
            for i, name in enumerate(("bk", "q_b", "k_b", "norm_w", "norm_b")):
                sp.dma_start(cols[:, i:i + 1], t_in[name]).then_inc(w_in, 16)
            sp.wait_ge(w_zero, 2)
            for e in range(SEG):
                m = D >> e
                sp.dma_start(o2w[0:m, e, 0:m], t_in["o_wT"][0:m, 0:m]).then_inc(w_in, 16)
                sp.dma_start(o2b[:, e, 0:m], t_in["o_b"][:, 0:m]).then_inc(w_in, 16)

            def load_unit(L, u):
                s, g = L.slot(u), u if L.one else u // 2
                rows16 = slice(16 * g, 16 * g + 16)
                sp.dma_start(keys[0:ROWS, s, :], k_dram[rows16].rearrange("r s t -> (r s) t")).then_inc(kv_in[s], 16)
                if L.one:
                    sp.dma_start(values[:, s, :], v1_all[:, g].rearrange("p a b c -> p (a b c)")).then_inc(kv_in[s], 16)
                else:
                    sp.dma_start(values[:, s, 0:TT * VW], v2_all[:, g].rearrange("p a b -> p (a b)")).then_inc(kv_in[s], 16)
                    sp.dma_start(queries[0:ROWS, s, :], q_dram[rows16].rearrange("r s t -> (r s) t")).then_inc(kv_in[s], 16)

            def load_positions(u):
                sp.dma_start(pos_b[:, u % 2], pos_dram[2 * u:2 * u + 2].rearrange("(o h) t -> o h t", o=1)
                             .broadcast_to([HALF, 2, T])).then_inc(pb_in[u % 2], 16)

            def guard_rows(b, L, u):
                sp.wait_ge(x_read, x_no(b, "guard", 1 if L.one else 2, u) + 1)
                s, q0 = L.slot(u), L.q0(u)
                for g in range(GUARD):
                    sp.dma_start(queries[ROWS + g:ROWS + g + 1, s, q0:q0 + L.nq].rearrange("p (a b) -> p a b", a=QTS),
                                 g_row[QTS * g:QTS * g + QTS, u % RING, 0:L.qw]).then_inc(guard_in[u % RING], 16)

            with sp.Fori(0, B) as b:
                sp.dma_start(xT[:, :], t_in["xT"][bass.ds(b, 1)].rearrange("b d t -> (b d) t")).then_inc(xT_in, 16)
                sp.dma_start(x_tok[:, :, :], t_in["x"][bass.ds(b, 1)].rearrange("b (a p) d -> (b p) a d", p=P)).then_inc(x_in, 16)
                sp.wait_ge(kp_rdy, b * 2 + 1)
                for s in range(SLOTS):
                    sp.dma_start(k_dram[:, s, :], k_part[K_SLOTS[s]][:, :]).then_inc(p_out, 16)
                sp.wait_ge(pos_rdy, b + 1)
                sp.dma_start(pos_dram, pos_row[0:P:8, :]).then_inc(pos_out, 16)
                sp.wait_ge(p_out, b * 288 + 96)
                sp.wait_ge(pos_out, b * 16 + 16)
                sp.sem_inc(s_hold, 1)
                sp.wait_ge(v_ev, b * 3 + 2)
                for u in range(3):
                    load_unit(L1, u)
                for u in range(2):
                    load_positions(u)
                for u in range(AHEAD):
                    guard_rows(b, L1, u)
                for u in range(L1.units):
                    if 0 < u and u + 3 < L1.units:
                        sp.wait_ge(pv_mm, tile_no(b, L1, u, 0))
                    if u + 3 < L1.units:
                        load_unit(L1, u + 3)
                    if u + AHEAD < L1.units:
                        guard_rows(b, L1, u + AHEAD)
                        sp.wait_ge(selt_v, b * PAIRS + u + 1)
                        sp.wait_ge(selt_p, b * PAIRS + u + 1)
                        load_positions(u + 2)
                sp.wait_ge(qp_rdy, b * 2 + 2)
                for s in range(SLOTS):
                    sp.dma_start(q_dram[:, s, :], q_part[Q_SLOTS[s]][:, :]).then_inc(p_out, 16)
                sp.wait_ge(kp_rdy, b * 2 + 2)
                for s in range(SLOTS):
                    sp.dma_start(k_dram[:, s, :], k_part[K_SLOTS[s]][:, :]).then_inc(p_out, 16)
                sp.wait_ge(p_out, b * 288 + 288)
                sp.sem_inc(s_hold, 1)
                sp.wait_ge(v_ev, b * 3 + 3)
                for u in (0, 2, 4):
                    load_unit(L2, u)
                for u in range(AHEAD):
                    guard_rows(b, L2, u)
                for u in range(L2.units):
                    if u % 2 == 0 and u + 6 < L2.units:
                        if u:
                            sp.wait_ge(pv_mm, tile_no(b, L2, u, 0))
                        load_unit(L2, u + 6)
                    if u + AHEAD < L2.units:
                        guard_rows(b, L2, u + AHEAD)
                sp.wait_ge(n_rdy, b * 3 + 3)
                sp.sem_inc(s_hold, 1)
                sp.dma_start(out[bass.ds(b, 1)].rearrange("b (a p) d -> (b p) a d", p=P), xh[:, :, :]).then_inc(y_out, 16)
                sp.wait_ge(y_out, b * 16 + 16)
                sp.sem_inc(s_hold, 1)

        @block.gpsimd
        def _(pool):
            pool.memset(o2w[:, :, :], 0.0).then_inc(w_zero, 1)
            pool.memset(o2b[:, :, :], 0.0).then_inc(w_zero, 1)
            pool.memset(ident[:, :], 0.0).then_inc(c_pool, 1)
            pool.memset(same_head[:, :], 1.0).then_inc(c_pool, 1)
            pool.iota(iota_i[:, :], pattern=[[1, TOP]], base=1, channel_multiplier=0).then_inc(c_pool, 1)
            pool.iota(iota_pi[:, :], pattern=[[HALF, 2]], base=1, channel_multiplier=1).then_inc(c_pool, 1)
            pool.iota(lane[:, :], pattern=[[0, 2]], base=0, channel_multiplier=1).then_inc(c_pool, 1)
            pool.wait_ge(c_pool, 5)
            pool.affine_select(ident[:, :], ident[:, :], [[-1, P]], ALU.not_equal, 1.0, 0, 1).then_inc(c_pool, 1)
            heads = same_head[:, :].rearrange("p (g c) -> p g c", c=8)
            pool.affine_select(heads, heads, [[-8, H1], [0, 8]], ALU.is_ge, 0.0, 0, 1).then_inc(c_pool, 1)
            pool.wait_ge(c_pool, 7)
            pool.affine_select(heads, heads, [[8, H1], [0, 8]], ALU.is_ge, 0.0, 7, -1).then_inc(c_pool, 1)

            def split(b, src, part, rdy, first):
                n = b * 12 + first
                pool.tensor_tensor(part[0][:, :], src[:, :], ones_t[:, :], ALU.mult).then_inc(p_step, 1)
                pool.wait_ge(p_step, n + 1)
                pool.tensor_tensor(rest[:, :], src[:, :], part[0][:, :], ALU.subtract).then_inc(p_step, 1)
                pool.wait_ge(p_step, n + 2)
                pool.tensor_tensor(part[1][:, :], rest[:, :], ones_t[:, :], ALU.mult).then_inc(p_step, 1)
                pool.wait_ge(p_step, n + 3)
                pool.tensor_tensor(part[2][:, :], rest[:, :], part[1][:, :], ALU.subtract).then_inc(rdy, 1)

            pool.wait_ge(c_rdy, 1)
            with pool.Fori(0, B) as b:
                pool.wait_ge(q_ev, 2 * b + 1)
                split(b, q32, q_part, qp_rdy, 0)
                pool.wait_ge(k_ev, 2 * b + 1)
                pool.wait_ge(qp_rdy, 2 * b + 1)
                split(b, k32, k_part, kp_rdy, 3)
                for u in range(L1.units):
                    pool.wait_ge(pb_in[u % 2], b * 64 + 16 * (u // 2 + 1))
                    if u >= 2:
                        pool.wait_ge(x_mm, x_no(b, "scatter", 1, u - 2) + 1)
                    pool.sem_inc(p_hold, 1)
                    pool.tensor_scalar(sel_t[:, u % 2, 1, 0, :], pos_b[:, u % 2, 1, :], iota_p[0:HALF, 0:1], None,
                                       ALU.is_equal)
                    pool.tensor_scalar(sel_t[:, u % 2, 1, 1, :], pos_b[:, u % 2, 1, :], iota_p[0:HALF, 1:2], None,
                                       ALU.is_equal).then_inc(selt_p, 1)
                pool.wait_ge(q_ev, 2 * b + 2)
                pool.wait_ge(qs_rdy, b * 12 + 12)
                pool.wait_ge(p_out, b * 288 + 96)
                split(b, q32, q_part, qp_rdy, 6)
                pool.wait_ge(k_ev, 2 * b + 2)
                pool.wait_ge(qp_rdy, 2 * b + 2)
                split(b, k32, k_part, kp_rdy, 9)

        @block.scalar
        def _(act):
            def exps(b, L, u, kt):
                n, ln = tile_no(b, L, u, kt), (L.u0 + u) * TT + kt
                act.wait_ge(score_mm, n + 1)
                if ln >= RING:
                    act.wait_ge(pv_mm, n - RING + 1)
                act.activation(probs[:, kt % RING, 0:L.nq], sbank[kt % 2][:, 0:L.nq], ACT.Exp,
                               scale=L.scale).then_inc(exp_done, 1)

            def copy_queries(b, u):
                act.wait_ge(x_mm, x_no(b, "gather", 1, u) + 1)
                if u >= RING:
                    act.wait_ge(score_mm, tile_no(b, L1, u - RING, TT - 1) + 1)
                act.activation(queries[0:ROWS, u % RING, 0:L1.nq], xbank[0:ROWS, 0:L1.nq], ACT.Copy).then_inc(x_read, 1)

            def copy_values(b, L, u):
                act.wait_ge(pv_mm, tile_no(b, L, u, TT - 1) + 1)
                if L.u0 + u >= 2:
                    act.wait_ge(x_mm, x_no(b, *turn_before(L, u)) + 1)
                act.activation(pv_sb[:, u % 2, 0:L.qw], vbank[:, 0:L.qw], ACT.Copy).then_inc(pv_ev, 1)

            def turn_before(L, u):
                n = 1 if L.one else 2
                return ("turn", n, u - 2) if u >= 2 else ("turn", 1, L1.units - 2 + u)

            def units(b, L):
                for u in range(L.units):
                    exps(b, L, u, 0)
                    if L.one and u + AHEAD < L.units:
                        copy_queries(b, u + AHEAD)
                    for kt in range(1, TT):
                        exps(b, L, u, kt)
                    copy_values(b, L, u)

            def deviation(b, i):
                act.wait_ge(sd_rdy, 3 * b + i + 1)
                act.activation(std[:, :], mv[:, :, 1], ACT.Sqrt, bias=eps_c[:, 0:1]).then_inc(rt_rdy, 1)

            act.wait_ge(c_rdy, 1)
            act.wait_ge(w_in, 16 * (7 + 4 + 5 + 2 * SEG))
            with act.Fori(0, B) as b:
                act.wait_ge(q_mm, 2 * b + 1)
                act.activation(q32[:, :], mbank[0][:, :], ACT.Copy).then_inc(q_ev, 1)
                act.wait_ge(k_mm, 2 * b + 1)
                act.activation(k32[:, :], mbank[1][:, :], ACT.Identity, bias=cols[:, 0:1]).then_inc(k_ev, 1)
                act.wait_ge(v_mm, 2 * b + 1)
                v_heads = mbank[0][:, :].rearrange("p (t g h d) -> p g t h d", g=PAIRS, h=2, d=HD1)
                for h in range(2):
                    act.activation(v1_all[:, :, :, h, 0:HD1], v_heads[:, :, :, h, :], ACT.Copy).then_inc(v_ev, 1)
                act.wait_ge(nt_mm, b + 1)
                act.activation(norms[:, :], mbank[1][:, :], ACT.Copy).then_inc(nt_ev, 1)
                act.wait_ge(qp_rdy, 2 * b + 1)
                to = q_slots[:, :, :, :].rearrange("p t (g h) (x d s) -> p (t g) h x d s", h=2, x=2, s=SLOTS)
                for s in range(SLOTS):
                    frm = q_part[Q_SLOTS[s]][:, :].rearrange("p (a h d) -> p a h d", h=2, d=HD1)
                    for h in range(2):
                        act.activation(to[:, :, h, h, :, s], frm[:, :, h, :], ACT.Copy).then_inc(qs_rdy, 1)
                for u in range(AHEAD):
                    copy_queries(b, u)
                units(b, L1)
                act.wait_ge(tr_mm, 3 * b + 1)
                act.activation(tr[:, :], mbank[0][:, :], ACT.Copy).then_inc(tr_ev, 1)
                deviation(b, 0)
                deviation(b, 1)
                act.wait_ge(tr_mm, 3 * b + 2)
                act.activation(tr[:, :], mbank[0][:, :], ACT.Identity, bias=cols[:, 4:5],
                               scale=cols[:, 3:4]).then_inc(tr_ev, 1)
                act.wait_ge(q_mm, 2 * b + 2)
                act.activation(q32[:, :], mbank[1][:, :], ACT.Identity, bias=cols[:, 1:2]).then_inc(q_ev, 1)
                act.wait_ge(k_mm, 2 * b + 2)
                act.activation(k32[:, :], mbank[0][:, :], ACT.Identity, bias=cols[:, 2:3]).then_inc(k_ev, 1)
                act.wait_ge(v_mm, 2 * b + 2)
                act.activation(v2_all[:, :, :, 0:HD2],
                               mbank[1][:, :].rearrange("p (t h d) -> p h t d", h=H2, d=HD2), ACT.Copy).then_inc(v_ev, 1)
                units(b, L2)
                act.wait_ge(tr_mm, 3 * b + 3)
                act.activation(tr[:, :], mbank[0][:, :], ACT.Copy).then_inc(tr_ev, 1)
                deviation(b, 2)

        @block.vector
        def _(dve):
            done = [0]
            STEPS = 158

            def own(b, ins):
                done[0] += 1
                ins.then_inc(v_step, 1)
                dve.wait_ge(v_step, b * STEPS + done[0])

            def last_own(b):
                dve.wait_ge(v_step, b * STEPS + done[0])

            dve.memset(ones_row[:, :], 1.0).then_inc(c_vec, 1)
            dve.memset(ones_t[:, :], 1.0).then_inc(c_vec, 1)
            dve.memset(eps_c[:, :], EPS).then_inc(c_vec, 1)
            dve.memset(keys[ROWS:KR, :, :], 1.0).then_inc(c_vec, 1)
            dve.memset(q_slots[:, :, :, :].rearrange("p a b c -> p (a b c)").bitcast(F32), 0.0).then_inc(c_vec, 1)
            dve.memset(v1_all[:, :, :, :, :], 0.0).then_inc(c_vec, 1)
            dve.memset(v2_all[:, :, :, :], 0.0).then_inc(c_vec, 1)
            dve.wait_ge(c_vec, 7)
            dve.memset(v1_all[:, :, :, :, HD1:HD1 + 1], 1.0).then_inc(c_vec, 1)
            dve.memset(v2_all[:, :, :, HD2:HD2 + 1], 1.0).then_inc(c_vec, 1)
            dve.wait_ge(c_pool, 8)
            dve.tensor_copy(ident_b[:, :], ident[:, :]).then_inc(c_vec, 1)
            dve.tensor_copy(iota_u[:, :], iota_i[:, :]).then_inc(c_vec, 1)
            dve.tensor_copy(iota_p[:, :], iota_pi[:, :]).then_inc(c_vec, 1)
            dve.tensor_scalar(lane[:, 1:2], lane[:, 0:1], 7, None, ALU.bitwise_and).then_inc(c_vec, 1)
            dve.wait_ge(c_vec, 13)
            for r in range(ROUNDS - 1):
                dve.tensor_scalar(digit[:, r:r + 1], lane[:, 1:2], SHIFTS[r], None, ALU.logical_shift_left).then_inc(c_vec, 1)
            dve.tensor_scalar(digit[:, ROUNDS - 1:], lane[:, 1:2], 1, None, ALU.min).then_inc(c_vec, 1)
            dve.wait_ge(c_vec, 13 + ROUNDS)
            dve.nop().then_inc(c_rdy, 1)

            def threshold(b):
                own(b, dve.memset(found[:, 0:1], 0))
                for r in range(ROUNDS):
                    own(b, dve.tensor_tensor(found[:, 1:2], found[:, 0:1], digit[:, r:r + 1], ALU.bitwise_or))
                    own(b, dve.tensor_scalar(cmp[:, :], norms[:, :], found[:, 1:2].bitcast(F32), None, ALU.is_ge,
                                             ALU.add, accum_out=count[:, 0:1]))
                    dve.tensor_scalar(count_b[:, :], count[:, 0:1], TOP - 0.5, None, ALU.is_ge).then_inc(cnt_rdy, 1)
                    dve.wait_ge(x_mm, x_no(b, "round", r) + 1)
                    ins = dve.tensor_scalar(count[:, 1:2], xbank[:, 0:1], -1.0, float(1 << SHIFTS[r]), ALU.add, ALU.mult)
                    ins.then_inc(x_read, 1)
                    dve.wait_ge(x_read, x_no(b, "round", r) + 1)
                    if r < ROUNDS - 1:
                        own(b, dve.tensor_copy(found[:, 2:3], count[:, 1:2]))
                    else:
                        own(b, dve.tensor_scalar(found[:, 2:3], count[:, 1:2], 1.0, None, ALU.min))
                    own(b, dve.tensor_tensor(found[:, 0:1], found[:, 0:1], found[:, 2:3], ALU.bitwise_or))

            def positions(b):
                limit = found[:, 0:1].bitcast(F32)
                own(b, dve.tensor_scalar(cmp[:, :], norms[:, :], limit, None, ALU.is_gt, ALU.add, accum_out=count[:, 0:1]))
                own(b, dve.tensor_scalar(count[:, 1:2], count[:, 0:1], -1.0, float(TOP), ALU.mult, ALU.add))
                own(b, dve.tensor_scalar(norms[:, :], norms[:, :], limit, None, ALU.is_equal))
                own(b, dve.tensor_tensor_scan(cum[:, :], ones_t[:, :], norms[:, :], 0.0, ALU.mult, ALU.add))
                own(b, dve.scalar_tensor_tensor(norms[:, :], cum[:, :], count[:, 1:2], norms[:, :], ALU.is_le, ALU.mult))
                own(b, dve.tensor_tensor(cmp[:, :], cmp[:, :], norms[:, :], ALU.add))
                own(b, dve.tensor_tensor_scan(cum[:, :], ones_t[:, :], cmp[:, :], 0.0, ALU.mult, ALU.add))
                dve.tensor_tensor(pos_row[:, :], cum[:, :], cmp[:, :], ALU.mult).then_inc(pos_rdy, 1)
                dve.wait_ge(x_mm, x_no(b, "position", 0) + 1)
                dve.tensor_copy(pos_col[:, :, :], xbank_b.rearrange("p (t h c) -> p t h c", t=TT, c=8)[:, :, :, 0])\
                   .then_inc(x_read, 1)
                dve.wait_ge(x_read, x_no(b, "position", 0) + 1)

            def build_sel(b, u):
                if u >= 2:
                    dve.wait_ge(x_mm, x_no(b, "gather", 1, u - 2) + 1)
                for h in range(2):
                    for t in range(TT):
                        ins = dve.tensor_scalar(sel[:, u % 2, h, t, :], iota_u[:, :], pos_col[:, t, 2 * u + h:2 * u + h + 1],
                                                None, ALU.is_equal)
                ins.then_inc(sel_rdy, 1)

            def build_sel_t(b, u):
                dve.wait_ge(pb_in[u % 2], b * 64 + 16 * (u // 2 + 1))
                if u >= 2:
                    dve.wait_ge(x_mm, x_no(b, "scatter", 1, u - 2) + 1)
                for half in range(2):
                    ins = dve.tensor_scalar(sel_t[:, u % 2, 0, half, :], pos_b[:, u % 2, 0, :],
                                            iota_p[0:HALF, half:half + 1], None, ALU.is_equal)
                ins.then_inc(selt_v, 1)

            def maxima(b, L, u):
                for q in range(QTS):
                    dve.wait_ge(max_mm, qt_no(b, L, u, q) + 1)
                    dve.tensor_reduce(mx[0:L.qw, q:q + 1], mbank[q % 2][0:L.qw, :], AX_X, ALU.max).then_inc(max_red, 1)
                dve.wait_ge(max_red, qt_no(b, L, u, QTS - 1) + 1)

            def guard_parts(b, L, u):
                n, w = 1 if L.one else 2, L.qw
                g = g_part[0:w, u % 2]
                if L.u0 + u >= 2:
                    dve.wait_ge(x_mm, x_no(b, "guard", *((n, u - 2) if u >= 2 else (1, L1.units - 2 + u))) + 1)
                own(b, dve.tensor_scalar(g[:, 0, :], mx[0:w, :], -1.0, None, ALU.mult))
                own(b, dve.scalar_tensor_tensor(mx_rest[0:w, :], mx[0:w, :], -1.0, g[:, 0, :], ALU.mult, ALU.subtract))
                dve.tensor_copy(g[:, 1, :], mx_rest[0:w, :]).then_inc(gp_rdy, 1)

            def guard_copy(b, L, u):
                dve.wait_ge(x_mm, x_no(b, "guard", 1 if L.one else 2, u) + 1)
                if L.u0 + u >= RING:
                    dve.wait_ge(guard_in[u % RING], guard_count(b, L, u) - 32)
                dve.tensor_copy(g_row[:, u % RING, 0:L.qw], xbank_b[0:GUARD * QTS, 0:L.qw]).then_inc(x_read, 1)

            def norm_outputs(b, L, u):
                w, d = L.qw, L.hd
                x = x_no(b, "turn", 1 if L.one else 2, u) + 1
                dve.wait_ge(x_mm, x)
                turned = xbank[0:w, 0:P].rearrange("p (g r) -> p g r", r=VW)
                own(b, dve.reciprocal(den[0:w, :], turned[:, :, d]))
                share = den[0:w, :].rearrange("p (g o) -> p g o", o=1).broadcast_to([w, QTS, d])
                if not L.one:
                    t0, c0 = QTS * (u % 2), HD2 * (u // 2)
                    dve.tensor_tensor(att[:, t0:t0 + QTS, c0:c0 + HD2], turned[:, :, 0:d], share, ALU.mult).then_inc(x_read, 1)
                    return
                dve.tensor_tensor(o_sel[:, :, :], turned[:, :, 0:d], share, ALU.mult).then_inc(x_read, 1)
                dve.wait_ge(x_read, x)
                parts = o_part[:, u % 2]
                if u >= 2:
                    dve.wait_ge(x_mm, x_no(b, "scatter", 1, u - 2) + 1)
                own(b, dve.tensor_copy(parts[:, :, 0, :], o_sel[:, :, :]))
                own(b, dve.tensor_tensor(o_rest[:, :, :], o_sel[:, :, :], parts[:, :, 0, :], ALU.subtract))
                own(b, dve.tensor_copy(parts[:, :, 1, :], o_rest[:, :, :]))
                dve.tensor_tensor(parts[:, :, 2, :], o_rest[:, :, :], parts[:, :, 1, :], ALU.subtract).then_inc(on_rdy, 1)

            def sum_scattered(b, u):
                dve.wait_ge(x_mm, x_no(b, "scatter", 1, u) + 1)
                x = xbank[:, 0:TT * 2 * 3 * HD1].rearrange("p (t h s d) -> p t h d s", t=TT, h=2, s=3)
                dve.tensor_reduce(att[:, :, 16 * u:16 * u + 8], x[:, :, 0], AX_X, ALU.add)
                dve.tensor_reduce(att[:, :, 16 * u + 8:16 * u + 16], x[:, :, 1], AX_X, ALU.add).then_inc(x_read, 1)

            def layernorm(b, src, dst, i):
                for t in range(TT):
                    ins = dve.bn_stats(stats[:, t, :], src[:, t, :])
                own(b, ins)
                dve.sem_inc(v_hold, 1)
                for t in range(TT):
                    ins = dve.bn_aggr(mv[:, t, :], stats[:, t, :])
                ins.then_inc(sd_rdy, 1)
                dve.wait_ge(rt_rdy, 3 * b + i + 1)
                own(b, dve.reciprocal(rstd[:, :], std[:, :]))
                for t in range(TT):
                    ins = dve.tensor_scalar(dst[:, t, :], src[:, t, :], mv[:, t, 0:1], rstd[:, t:t + 1],
                                            ALU.subtract, ALU.mult)
                ins.then_inc(n_rdy, 1)
                dve.wait_ge(n_rdy, 3 * b + i + 1)

            with dve.Fori(0, B) as b:
                done[0] = 0
                dve.wait_ge(q_ev, 2 * b + 1)
                own(b, dve.tensor_tensor(cum[:, :], q32[:, :], q32[:, :], ALU.mult))
                own(b, dve.tensor_reduce(n2[:, :], cum[:, :].rearrange("p (a d) -> p a d", d=HD1), AX_X, ALU.add))
                dve.tensor_copy(n2rep[:, :, :, :].rearrange("p t h c -> p (t h) c"),
                                n2[:, :].rearrange("p (a o) -> p a o", o=1).broadcast_to([P, TT * H1, 8])).then_inc(n2_rdy, 1)
                dve.wait_ge(nt_ev, b + 1)
                threshold(b)
                positions(b)
                for u in range(2):
                    build_sel(b, u)
                for u in range(AHEAD):
                    maxima(b, L1, u)
                    guard_parts(b, L1, u)
                for u in range(AHEAD):
                    guard_copy(b, L1, u)
                build_sel(b, 2)
                for u in range(L1.units + 1):
                    if u < L1.units:
                        build_sel_t(b, u)
                    if u > 0:
                        norm_outputs(b, L1, u - 1)
                    if u + 3 < L1.units:
                        build_sel(b, u + 3)
                    if u + AHEAD < L1.units:
                        maxima(b, L1, u + AHEAD)
                    if u > 0:
                        sum_scattered(b, u - 1)
                    if u + AHEAD < L1.units:
                        guard_parts(b, L1, u + AHEAD)
                        guard_copy(b, L1, u + AHEAD)
                dve.wait_ge(z_mm, 2 * b + 1)
                dve.wait_ge(x_in, 16 * b + 16)
                own(b, dve.tensor_tensor(zt[:, :, :].rearrange("p t d -> p (t d)"), mbank[1][:, :],
                                         x_tok[:, :, :].rearrange("p t d -> p (t d)"), ALU.add))
                layernorm(b, zt, x1, 0)
                layernorm(b, x1, xh, 1)
                for u in range(L2.units + 1 + AHEAD):
                    v = u - AHEAD
                    if v > 0:
                        norm_outputs(b, L2, v - 1)
                    if u < L2.units:
                        maxima(b, L2, u)
                        guard_parts(b, L2, u)
                    if 0 <= v and u < L2.units:
                        guard_copy(b, L2, u)
                    if v == -1:
                        guard_copy(b, L2, 0)
                        guard_copy(b, L2, 1)
                dve.wait_ge(z_mm, 2 * b + 2)
                own(b, dve.scalar_tensor_tensor(zt[:, :, :].rearrange("p t d -> p (t d)"),
                                                x1[:, :, :].rearrange("p t d -> p (t d)"), 2.0, mbank[1][:, :],
                                                ALU.mult, ALU.add))
                layernorm(b, zt, xh, 2)
                assert done[0] == STEPS, done[0]

        @block.tensor
        def _(pe):
            def with_row(dst, lhsT, rhs, bias):
                pe.matmul(dst, lhsT, rhs, start=True, stop=False)
                return pe.matmul(dst, ones_row[:, :], bias, start=False, stop=True)

            def tile(bank, t, w=P):
                return bank[:, t * w:t * w + w]

            def turn_all(bank, src):
                for t in range(TT):
                    ins = pe.transpose(tile(bank, t), src(t), ident[:, :])
                return ins

            def small_bank(b, *key):
                if X_PLAN[key]:
                    pe.wait_ge(x_read, x_no(b, *key))

            def gather(b, u):
                small_bank(b, "gather", 1, u)
                pe.wait_ge(sel_rdy, b * PAIRS + u + 1)
                for h in range(2):
                    for t in range(TT):
                        ins = pe.matmul(xbank[0:ROWS, h * TOP:h * TOP + TOP], q_slots[:, t, 2 * u + h, :],
                                        sel[:, u % 2, h, t, :], start=(t == 0), stop=(t == TT - 1))
                ins.then_inc(x_mm, 1)

            def max_scores(b, L, u, q):
                i, s = qt_no(b, L, u, q), L.slot(u)
                if q == 0:
                    pe.wait_ge(kv_in[s], kv_count(b, L, u))
                    if L.one:
                        pe.wait_ge(x_read, x_no(b, "gather", 1, u) + 1)
                if (L.u0 + u) * QTS + q >= 2:
                    pe.wait_ge(max_red, i - 1)
                c0 = L.q0(u) + q * L.qw
                for c in range(2):
                    ins = pe.matmul(mbank[q % 2][0:L.qw, c * 512:c * 512 + 512], queries[0:ROWS, s, c0:c0 + L.qw],
                                    keys[0:ROWS, s, c * 512:c * 512 + 512], start=True, stop=True)
                ins.then_inc(max_mm, 1)

            def turn_guard(b, L, u):
                small_bank(b, "guard", 1 if L.one else 2, u)
                pe.wait_ge(gp_rdy, unit_no(b, L, u) + 1)
                pe.transpose(xbank_b[0:GUARD * QTS, 0:L.qw],
                             g_part[0:L.qw, u % 2].rearrange("p a b -> p (a b)"),
                             ident_b[0:L.qw, 0:L.qw]).then_inc(x_mm, 1)

            def scores(b, L, u, kt):
                s, ln = L.slot(u), (L.u0 + u) * TT + kt
                if kt == 0:
                    pe.wait_ge(guard_in[u % RING], guard_count(b, L, u))
                if ln >= 2:
                    pe.wait_ge(exp_done, tile_no(b, L, u, kt) - 1)
                q0 = L.q0(u)
                pe.matmul(sbank[kt % 2][:, 0:L.nq], keys[:, s, kt * P:kt * P + P],
                          queries[:, s, q0:q0 + L.nq], start=True, stop=True).then_inc(score_mm, 1)

            def add_values(b, L, u, kt):
                pe.wait_ge(exp_done, tile_no(b, L, u, kt) + 1)
                if kt == 0 and L.u0 + u:
                    pe.wait_ge(pv_ev, unit_no(b, L, u))
                s, w = L.slot(u), L.qw
                for g in range(QTS):
                    c = (kt * 2 + g // 2) * VW if L.one else kt * VW
                    ins = pe.matmul(vbank[VW * g:VW * g + VW, 0:w], values[:, s, c:c + VW],
                                    probs[:, kt % RING, g * w:g * w + w], start=(kt == 0), stop=(kt == TT - 1))
                ins.then_inc(pv_mm, 1)

            def turn_outputs(b, L, u):
                small_bank(b, "turn", 1 if L.one else 2, u)
                pe.wait_ge(pv_ev, unit_no(b, L, u) + 1)
                pe.transpose(xbank[0:L.qw, 0:P], pv_sb[:, u % 2, 0:L.qw], ident[:, :]).then_inc(x_mm, 1)

            def scatter(b, u):
                small_bank(b, "scatter", 1, u)
                pe.wait_ge(on_rdy, b * PAIRS + u + 1)
                pe.wait_ge(selt_v, b * PAIRS + u + 1)
                pe.wait_ge(selt_p, b * PAIRS + u + 1)
                for t in range(TT):
                    for h in range(2):
                        c = (t * 2 + h) * 3 * HD1
                        for half in range(2):
                            ins = pe.matmul(xbank[:, c:c + 3 * HD1], sel_t[:, u % 2, h, half, t * P:t * P + P],
                                            o_part[:, u % 2, 2 * h + half].rearrange("p s d -> p (s d)"),
                                            start=(half == 0), stop=(half == 1))
                ins.then_inc(x_mm, 1)

            def units(b, L):
                for u in range(AHEAD):
                    for q in range(QTS):
                        max_scores(b, L, u, q)
                for u in range(AHEAD):
                    turn_guard(b, L, u)
                for u in range(L.units + 1):
                    ahead = u + AHEAD < L.units
                    for kt in range(TT):
                        if u < L.units:
                            scores(b, L, u, kt)
                        if kt == 0 and L.one and ahead:
                            gather(b, u + AHEAD)
                        if 0 < kt and u < L.units:
                            add_values(b, L, u, kt - 1)
                        if kt == 2 and u > 0:
                            turn_outputs(b, L, u - 1)
                        if 2 <= kt < 2 + QTS and ahead:
                            max_scores(b, L, u + AHEAD, kt - 2)
                        if kt == 5 and u > 0 and L.one:
                            scatter(b, u - 1)
                    if u < L.units:
                        add_values(b, L, u, TT - 1)
                    if ahead:
                        turn_guard(b, L, u + AHEAD)

            pe.wait_ge(c_rdy, 1)
            pe.wait_ge(w_in, 16 * (7 + 4 + 5 + 2 * SEG))
            with pe.Fori(0, B) as b:
                pe.wait_ge(xT_in, 16 * b + 16)
                for t in range(TT):
                    ins = with_row(tile(mbank[0], t), tile(xT, t), wqT[:, :], rows[:, 0, :])
                ins.then_inc(q_mm, 1)
                for c in range(2):
                    ins = pe.matmul(tile(mbank[1], c, 512), wkT[:, :], tile(xT, c, 512), start=True, stop=True)
                ins.then_inc(k_mm, 1)
                pe.wait_ge(q_ev, 2 * b + 1)
                for t in range(TT):
                    ins = with_row(tile(mbank[0], t), tile(xT, t), wvT[:, :], rows[:, 1, :])
                ins.then_inc(v_mm, 1)
                pe.wait_ge(k_ev, 2 * b + 1)
                pe.wait_ge(n2_rdy, b + 1)
                turn_all(mbank[1], lambda t: n2rep[:, t].rearrange("p h c -> p (h c)")).then_inc(nt_mm, 1)
                for r in range(ROUNDS):
                    small_bank(b, "round", r)
                    pe.wait_ge(cnt_rdy, b * ROUNDS + r + 1)
                    pe.matmul(xbank[:, 0:1], same_head[:, :], count_b[:, :], start=True, stop=True).then_inc(x_mm, 1)
                small_bank(b, "position", 0)
                pe.wait_ge(pos_rdy, b + 1)
                for t in range(TT):
                    ins = pe.transpose(tile(xbank_b, t), tile(pos_row, t), ident_b[:, :])
                ins.then_inc(x_mm, 1)
                pe.wait_ge(qs_rdy, 12 * b + 12)
                for u in range(AHEAD):
                    gather(b, u)
                pe.wait_ge(v_ev, 3 * b + 2)
                pe.wait_ge(nt_ev, b + 1)
                units(b, L1)
                pe.wait_ge(x_read, x_no(b, "scatter", 1, L1.units - 1) + 1)
                turn_all(mbank[0], lambda t: att[:, t, :]).then_inc(tr_mm, 1)
                pe.wait_ge(tr_ev, 3 * b + 1)
                for t in range(TT):
                    ins = with_row(tile(mbank[1], t), tile(tr, t), woT[:, :], rows[:, 2, :])
                ins.then_inc(z_mm, 1)
                pe.wait_ge(n_rdy, 3 * b + 2)
                turn_all(mbank[0], lambda t: xh[:, t, :]).then_inc(tr_mm, 1)
                pe.wait_ge(tr_ev, 3 * b + 2)
                for bank, w, done in ((mbank[1], q2w, q_mm), (mbank[0], k2w, k_mm)):
                    for e in range(SEG):
                        m, c = D >> e, T // SEG
                        ins = pe.matmul(tile(bank, e, c), w[0:m, :], tr[0:m, e * c:e * c + c], start=True, stop=True)
                    ins.then_inc(done, 1)
                pe.wait_ge(q_ev, 2 * b + 2)
                for t in range(TT):
                    m = D >> (t * SEG // TT)
                    ins = with_row(tile(mbank[1], t), tr[0:m, t * P:t * P + P], v2w[0:m, :], rows[:, 3, :])
                ins.then_inc(v_mm, 1)
                pe.wait_ge(v_ev, 3 * b + 3)
                pe.wait_ge(k_ev, 2 * b + 2)
                units(b, L2)
                pe.wait_ge(x_read, b * X_USES + X_USES)
                turn_all(mbank[0], lambda t: att[:, t, :]).then_inc(tr_mm, 1)
                pe.wait_ge(tr_ev, 3 * b + 3)
                for t in range(TT):
                    e = t * SEG // TT
                    m = D >> e
                    ins = with_row(tile(mbank[1], t), tr[0:m, t * P:t * P + P], o2w[0:m, e, :], o2b[:, e, :])
                ins.then_inc(z_mm, 1)


_TURNED = {"WqT": "L0_attn_Wq", "WkT": "L0_attn_Wk", "WvT": "L0_attn_Wv", "WoT": "L0_attn_Wo",
           "q_wT": "L0_ffn_q_w", "k_wT": "L0_ffn_k_w", "v_wT": "L0_ffn_v_w", "o_wT": "L0_ffn_o_w"}
_ROWS = {"bq": "L0_attn_bq", "bv": "L0_attn_bv", "bo": "L0_attn_bo", "v_b": "L0_ffn_v_b", "o_b": "L0_ffn_o_b"}
_COLS = {"bk": "L0_attn_bk", "q_b": "L0_ffn_q_b", "k_b": "L0_ffn_k_b", "norm_w": "L0_ffn_norm_w",
         "norm_b": "L0_ffn_norm_b"}


def kernel(**inputs):
    import numpy as _np
    import concourse.bacc as _bacc
    from concourse.bass_utils import run_bass_kernel_spmd as _run

    nc = _bacc.Bacc("TRN2", target_bir_lowering=False, num_devices=1)
    x = _np.asarray(inputs["L0_attn_x"])
    given = {"x": x, "xT": x.transpose(0, 2, 1)}
    given |= {k: _np.asarray(inputs[n]).T for k, n in _TURNED.items()}
    given |= {k: _np.asarray(inputs[n]).reshape(1, D) for k, n in _ROWS.items()}
    given |= {k: _np.asarray(inputs[n]).reshape(D, 1) for k, n in _COLS.items()}
    arrays, t_in = {}, {}
    for name, a in given.items():
        a = _np.ascontiguousarray(a)
        arrays[f"in_{name}"] = a
        t_in[name] = nc.dram_tensor(f"in_{name}", a.shape, F32, kind="ExternalInput").ap()
    out = nc.dram_tensor("out", (B, T, D), F32, kind="ExternalOutput").ap()
    build(nc, t_in, out)
    r = _run(nc, [arrays], core_ids=[0])
    return r.results[0]["out"]
```

```python
from contextlib import ExitStack

import concourse.bass as bass
from concourse import mybir

ALU = mybir.AluOpType
ACT = mybir.ActivationFunctionType
AX_X = mybir.AxisListType.X
F32 = mybir.dt.float32
BF16 = mybir.dt.bfloat16
I32 = mybir.dt.int32

P = 128
B = 4
T = 1024
D = 128
TT = T // P
EPS = 1e-5

H1 = 16
HD1 = D // H1
TOP = T // 5
HALF = TOP // 2
PAIRS = H1 // 2

H2 = 8
HD2 = D // H2
SEG = 4

K_SLOTS = (0, 1, 0, 1, 2, 0)
Q_SLOTS = (0, 0, 1, 1, 0, 2)
SLOTS = len(K_SLOTS)
ROWS = 16 * SLOTS
GUARD = 2
KR = ROWS + GUARD
VW = 32

QTS = 4
RING = 4
AHEAD = 2

SHIFTS = tuple(range(28, 0, -3)) + (0,)
ROUNDS = len(SHIFTS)


class Layer:

    def __init__(self, index):
        self.one = index == 1
        self.units = PAIRS if self.one else 2 * H2
        self.u0 = 0 if self.one else PAIRS
        self.qw = HALF if self.one else P
        self.nq = QTS * self.qw
        self.scale = HD1 ** -0.5 if self.one else D ** -0.5
        self.hd = HD1 if self.one else HD2

    def slot(self, u):
        return (u if self.one else u // 2) % RING

    def q0(self, u):
        return 0 if self.one else u % 2 * self.nq


L1, L2 = Layer(1), Layer(2)

BANK_STEPS = {"q", "k", "v", "norm", "round", "position", "at", "y", "xt", "q2", "k2", "v2", "ft", "fo"}

PREPARE = ([(0, "q", 0), (1, "q", 1), (2, "squares", 0), (2, "k", 0), (3, "k", 1), (4, "norm", 0), (5, "norm", 1)]
           + [(6 + r, "round", r) for r in range(ROUNDS)]
           + [(17, "positions", 0), (17, "v", 0), (18, "v", 1), (19, "position", 0)]
           + [(21 + s // 2, "spread", s) for s in range(SLOTS)])
BETWEEN_1 = [(0, "at", 0), (1, "at", 1), (2, "y", 0), (3, "y", 1), (4, "norm1", 0), (8, "norm2", 0), (12, "norm3", 0),
             (13, "xt", 0), (14, "xt", 1), (15, "q2", 0), (16, "q2", 1), (17, "k2", 0), (18, "k2", 1),
             (19, "v2", 0), (20, "v2", 1)]
BETWEEN_2 = [(0, "at", 0), (1, "at", 1), (2, "y", 0), (3, "y", 1), (4, "norm1", 0), (7, "norm2", 0), (10, "norm3", 0),
             (11, "xt", 0), (12, "xt", 1), (13, "q2", 0), (14, "q2", 1), (15, "k2", 0), (16, "k2", 1),
             (21, "v2", 0), (22, "v2", 1)]
FINISH = [(5, "ft", 0), (6, "ft", 1), (8, "fo", 0), (9, "fo", 1), (11, "norm4", 0), (14, "norm5", 0)]

SEL_VECTOR, SEL_VECTOR_ALONE = 6, 12
VECTOR_STEPS = {"first": 56, "loop1": 102, "last1": 50, "head2": 50, "loop2": 51, "last2": 47, "end": 1}


class Segment:

    def __init__(self, name, before, times, layer=None, after=None, prepare=False, between=False, finish=False):
        self.name, self.layer, self.next_layer = name, layer, after
        self.prepare, self.between, self.finish = prepare, between, finish
        self.units = n = layer.units if layer else 0
        self.slot_kt = (1, 4, 6, 7) if layer is L1 else (1, 5)
        self.slots = len(self.slot_kt)
        self.steps = {}
        for on, todo in ((prepare, PREPARE), (between, BETWEEN_1 if layer is L1 else BETWEEN_2), (finish, FINISH)):
            for slot, step, i in todo if on else ():
                self.steps.setdefault(slot, []).append((step, i))
        order = []
        if layer is None:
            order += [x for slot in sorted(self.steps) for x in self.steps[slot]]
            order += [("gather", 0), ("gather", 1), ("guard", 0)] if after else []
        for u in range(n):
            at = [self.steps.get(u * self.slots + j, []) for j in range(self.slots)]
            guard = [("guard", u + 1)] if self.has(u + 1) else []
            turn = [("turn", u - 1)] if u else []
            if layer.one:
                if u + AHEAD < n or after is L1:
                    order += [("gather", u + AHEAD)]
                order += at[0] + guard + turn + at[1] + ([("scatter", u - 1)] if u else []) + at[2] + at[3]
            else:
                order += at[0] + guard + turn + at[1]
        if layer:
            order += [("turn", n - 1)] + ([("scatter", n - 1)] if layer.one else [])
        bank = {"gather", "guard", "turn", "scatter"} | BANK_STEPS
        uses = [x for x in order if x[0] in bank]
        self.index = {key: i for i, key in enumerate(uses)}
        self.uses, self.before, self.times = len(uses), before, times
        self.after = before + times * len(uses)

    def has(self, u):
        return u < self.units or self.next_layer is not None

    def unit(self, u):
        if u < self.units:
            return self.layer, self.batch, u
        if self.next_layer is self.layer:
            return self.layer, self.batch + 1, u - self.units
        return self.next_layer, 0, u - self.units

    def loads(self, u):
        n = self.units
        if self.layer.one:
            if u + 3 < n or self.next_layer is L1:
                return [u + 3]
            return [n + 2 * (u - 6)] if u >= 6 else []
        return [u + 4] if u % 2 == 0 and self.has(u + 4) else []

    def x0(self):
        return self.it * self.uses + self.before

    def at(self, it, batch, other=None, done=None):
        self.it, self.batch, self.other, self.done = it, batch, other, done
        return self

    def x(self, *key):
        return self.it * self.uses + (self.before + self.index[key])


def segments():
    plan = [("first", 1, {"after": L1, "prepare": True}),
            ("loop1", B - 1, {"layer": L1, "after": L1, "prepare": True}),
            ("last1", 1, {"layer": L1, "after": L2, "between": True}),
            ("head2", 1, {"layer": L2, "after": L2, "between": True}),
            ("loop2", B - 2, {"layer": L2, "after": L2, "between": True, "finish": True}),
            ("last2", 1, {"layer": L2, "finish": True}),
            ("end", 1, {"finish": True})]
    out, before = [], 0
    for name, times, what in plan:
        out.append(Segment(name, before, times, **what))
        before = out[-1].after
    return out


def run(engine, body):
    first, loop1, last1, head2, loop2, last2, end = segments()
    body(first.at(0, None, 0))
    with engine.Fori(0, B - 1) as i:
        body(loop1.at(i, i, i + 1))
    body(last1.at(0, B - 1, 0))
    body(head2.at(0, 0, 1))
    with engine.Fori(0, B - 2) as i:
        body(loop2.at(i, i + 1, i + 2, i))
    body(last2.at(0, B - 1, None, B - 2))
    body(end.at(0, None, None, B - 1))


def build(nc, t_in, out):
    ctx = ExitStack()
    with ctx:
        def sb(name, shape, dt=F32):
            return ctx.enter_context(nc.sbuf_tensor(name, shape, dt))

        def ps(name, shape, dt=F32):
            return ctx.enter_context(nc.psum_tensor(name, shape, dt))

        def sem(name):
            return ctx.enter_context(nc.semaphore(name))

        def dram(name, shape, dt):
            return nc.dram_tensor(name, shape, dt, kind="Internal").ap()

        k1_dram = dram("k1_parts", (B, D, SLOTS, T), BF16)
        k2_dram = dram("k2_parts", (B, D, SLOTS, T), BF16)
        q2_dram = dram("q2_parts", (B, D, SLOTS, T), BF16)
        pos_dram = dram("positions", (B, H1, T), BF16)
        att1_dram = dram("attention1", (B, P, TT * D), F32)
        att2_dram = dram("attention2", (B, P, TT * D), F32)
        x1_dram = dram("x1_tokens", (B, P, TT * D), F32)

        wqT, wkT, wvT, woT = (sb(n, [P, D]) for n in ("wqT", "wkT", "wvT", "woT"))
        q2w, k2w, v2w = (sb(n, [P, D]) for n in ("q2w", "k2w", "v2w"))
        o2w = sb("o2w", [P, SEG, D])
        rows = sb("rows", [1, 4, D])
        o2b = sb("o2b", [1, SEG, D])
        cols = sb("cols", [P, 5])
        ones_row = sb("ones_row", [1, P])
        ident = sb("ident", [P, P])
        ident_b = sb("ident_b", [P, P], BF16)
        same_head = sb("same_head", [P, P], BF16)
        iota_u = sb("iota_u", [P, TOP], BF16)
        iota_i = sb("iota_i", [P, TOP], I32)
        iota_p = sb("iota_p", [P, 2])
        iota_pi = sb("iota_pi", [P, 2], I32)
        lane = sb("lane", [P, 2], I32)
        digit = sb("digit", [P, ROUNDS], I32)
        ones_t = sb("ones_t", [P, T])

        xT = sb("xT", [P, T])
        x_tok = sb("x_tok", [P, TT, D])
        q32 = sb("q32", [P, T])
        k32 = sb("k32", [P, T])
        n2 = sb("n2", [P, TT * H1])
        norms = sb("norms", [P, T])
        cmp = sb("cmp", [P, T])
        cum = sb("cum", [P, T])
        n2rep = cmp[:, :].rearrange("p (t h c) -> p t h c", t=TT, c=8)
        pos_row = sb("pos_row", [P, T], BF16)
        pos_col = sb("pos_col", [P, TT, H1])
        found = sb("found", [P, 3], I32)
        count = sb("count", [P, 2])
        count_b = sb("count_b", [P, 1], BF16)
        rest = sb("rest", [P, T])
        k_part = [sb(f"k_part{i}", [P, T], BF16) for i in range(3)]
        q_part = [sb(f"q_part{i}", [P, T], BF16) for i in range(3)]
        q_slots = sb("q_slots", [P, TT, H1, ROWS], BF16)
        v1_all = sb("v1_all", [P, PAIRS, TT, 2, VW])
        v2_all = sb("v2_all", [P, H2, TT, VW])
        att = sb("att", [P, TT, D])
        x1 = sb("x1", [P, TT, D])
        tr = sb("tr", [P, T])
        att_in = sb("att_in", [P, TT, D])
        fin_in = sb("fin_in", [P, TT, D])
        x1_in = norms[:, :].rearrange("p (t d) -> p t d", t=TT)
        fin_tr = xT
        zt, xh, y_sb = x_tok, att_in, fin_in
        stats = sb("stats", [P, TT, 6])
        mv = sb("mv", [P, TT, 2])
        var = sb("var", [P, TT])
        rstd = sb("rstd", [P, TT])
        eps_t = sb("eps_t", [P, TT])
        power = sb("power", [P, TT])

        keys = sb("keys", [KR, RING, T], BF16)
        queries = sb("queries", [KR, RING, T], BF16)
        values = sb("values", [P, RING, TT * 2 * VW])
        sel = sb("sel", [P, 2, 2, TT, TOP], BF16)
        sel_t = sb("sel_t", [HALF, 2, 2, 2, T], BF16)
        pos_b = sb("pos_b", [HALF, 2, 2, T], BF16)
        probs = sb("probs", [P, RING, 512])
        mx = sb("mx", [P, 2, QTS])
        mx_rest = sb("mx_rest", [P, QTS])
        g_part = sb("g_part", [P, 2, GUARD, QTS], BF16)
        g_row = sb("g_row", [GUARD * QTS, RING, P], BF16)
        pv_sb = sb("pv_sb", [P, 2, P])
        den = sb("den", [P, QTS])
        o_sel = sb("o_sel", [HALF, QTS, HD1])
        o_rest = sb("o_rest", [HALF, QTS, HD1])
        o_part = sb("o_part", [HALF, 2, QTS, 3, HD1], BF16)

        mbank = [ps(f"mbank{i}", [P, 1024]) for i in range(2)]
        sbank = [ps(f"sbank{i}", [P, 512]) for i in range(2)]
        vbank = ps("vbank", [P, 512])
        xbank = ps("xbank", [P, 512])
        xbank_b = xbank[:, :].bitcast(BF16)

        w_in, w_zero = sem("weights_loaded"), sem("weights_zeroed")
        c_pool, c_vec, c_rdy = sem("constants_pool"), sem("constants_vector"), sem("constants_ready")
        xT_in, mid_in, fin_in_s = sem("xT_loaded"), sem("between_loaded"), sem("finish_loaded")
        n2_rdy, cnt_rdy, pos_rdy = sem("norms_ready"), sem("count_ready"), sem("positions_ready")
        pos_out = sem("positions_stored")
        qp_rdy, kp_rdy, qs_rdy = sem("q_parts_ready"), sem("k_parts_ready"), sem("q_slots_ready")
        k1_out, qk2_out = sem("k1_parts_stored"), sem("second_parts_stored")
        p_step, v_step = sem("pool_step"), sem("vector_step")
        kv_in = [sem(f"unit_loaded{i}") for i in range(RING)]
        pb_in = [sem(f"position_rows_loaded{i}") for i in range(2)]
        sel_v, sel_p, selt_v = sem("sel_vector"), sem("sel_pool"), sem("sel_t_ready")
        max_mm, max_red = sem("max_scores"), sem("max_reduced")
        gp_rdy, on_rdy = sem("guard_parts"), sem("outputs_normed")
        x_mm, x_read = sem("small_bank_written"), sem("small_bank_read")
        guard_in = [sem(f"guard_rows_loaded{i}") for i in range(RING)]
        score_mm, exp_done, pv_mm, pv_ev = sem("scores"), sem("exponentials"), sem("values_added"), sem("values_copied")
        att_out, p_var = sem("attention_stored"), sem("variance_eps")
        x1_rdy, x1_out, xh_rdy = sem("x1_ready"), sem("x1_stored"), sem("x_hat_ready")
        sd_rdy, rt_rdy = sem("variance_ready"), sem("deviation_ready")
        y_rdy, y_out = sem("output_ready"), sem("output_stored")
        p_hold, v_hold, s_hold = sem("pool_hold"), sem("vector_hold"), sem("dma_hold")

        FREE_S, FREE_M, FREE_P, FREE_V, FREE_A = 2, 2, RING, 1, 16

        def unit_no(b, L, u):
            return b * 8 + u if L.one else b * 16 + (B * 8 + u)

        def tile_no(b, L, u, kt):
            return b * (8 * TT) + (u * TT + kt) if L.one else b * (16 * TT) + ((B * 8 + u) * TT + kt)

        def qt_no(b, L, u, q):
            return b * (8 * QTS) + (u * QTS + q) if L.one else b * (16 * QTS) + ((B * 8 + u) * QTS + q)

        def kv_count(b, L, u):
            return b * 64 + 32 * (u // RING + 1) if L.one else b * 96 + (B * 64 + 48 * (u // 2 // RING + 1))

        def guard_count(b, L, u):
            return b * 64 + 32 * (u // RING + 1) if L.one else b * 128 + (B * 64 + 32 * (u // RING + 1))

        def att_stored(b, L):
            return b * 16 + (FREE_A if L.one else 16 * B + FREE_A)

        def norm_no(seg, which):
            first = {"last1": 0, "head2": 2, "loop2": 4, "last2": 2 * B, "end": 2 * B + 1}[seg.name]
            if seg.name == "loop2":
                return seg.it * 3 + (first + which)
            if seg.name in ("last2", "end"):
                return first + (B - 2)
            return first + which

        def dve_tiles(seg):
            return SEL_VECTOR_ALONE if seg.layer is None else SEL_VECTOR

        def slot_read(engine, seg, u):
            if u >= 3 and ("gather", u - 2) not in seg.index:
                engine.wait_ge(x_mm, seg.x0())
            elif u >= 2 or seg.units:
                engine.wait_ge(x_mm, seg.x("gather", u - 2) + 1)

        block = ctx.enter_context(nc.Block())

        @block.sync
        def _(sp):
            for dst, name in ((wqT, "WqT"), (wkT, "WkT"), (wvT, "WvT"), (woT, "WoT"),
                              (q2w, "q_wT"), (k2w, "k_wT"), (v2w, "v_wT")):
                sp.dma_start(dst[:, :], t_in[name]).then_inc(w_in, 16)
            for i, name in enumerate(("bq", "bv", "bo", "v_b")):
                sp.dma_start(rows[:, i, :], t_in[name]).then_inc(w_in, 16)
            for i, name in enumerate(("bk", "q_b", "k_b", "norm_w", "norm_b")):
                sp.dma_start(cols[:, i:i + 1], t_in[name]).then_inc(w_in, 16)
            sp.sem_inc(att_out, FREE_A)
            sp.wait_ge(w_zero, 2)
            for e in range(SEG):
                m = D >> e
                sp.dma_start(o2w[0:m, e, 0:m], t_in["o_wT"][0:m, 0:m]).then_inc(w_in, 16)
                sp.dma_start(o2b[:, e, 0:m], t_in["o_b"][:, 0:m]).then_inc(w_in, 16)

            def one(dram, b):
                return dram[bass.ds(b, 1)]

            def heads16(dram, b, g):
                return one(dram, b)[:, 16 * g:16 * g + 16].rearrange("b r s t -> (b r s) t")

            def tokens(dram, b):
                return one(dram, b).rearrange("b (a p) d -> (b p) a d", p=P)

            def held(sem_, value):
                sp.wait_ge(sem_, value)
                sp.sem_inc(s_hold, 1)

            def load_unit(L, b, u):
                s, g = L.slot(u), u if L.one else u // 2
                if L.one:
                    sp.dma_start(keys[0:ROWS, s, :], heads16(k1_dram, b, g)).then_inc(kv_in[s], 16)
                    sp.dma_start(values[:, s, :], v1_all[:, g].rearrange("p a b c -> p (a b c)")).then_inc(kv_in[s], 16)
                else:
                    sp.dma_start(keys[0:ROWS, s, :], heads16(k2_dram, b, g)).then_inc(kv_in[s], 16)
                    sp.dma_start(values[:, s, 0:TT * VW], v2_all[:, g].rearrange("p a b -> p (a b)")).then_inc(kv_in[s], 16)
                    sp.dma_start(queries[0:ROWS, s, :], heads16(q2_dram, b, g)).then_inc(kv_in[s], 16)

            def load_positions(b, u):
                sp.dma_start(pos_b[:, u % 2], one(pos_dram, b)[:, 2 * u:2 * u + 2].broadcast_to([HALF, 2, T]))\
                  .then_inc(pb_in[u % 2], 16)

            def guard_rows(seg, u):
                sp.wait_ge(x_read, seg.x("guard", u) + 1)
                L, b, v = seg.unit(u)
                s, q0 = L.slot(v), L.q0(v)
                for g in range(GUARD):
                    sp.dma_start(queries[ROWS + g:ROWS + g + 1, s, q0:q0 + L.nq].rearrange("p (a b) -> p a b", a=QTS),
                                 g_row[QTS * g:QTS * g + QTS, v % RING, 0:L.qw]).then_inc(guard_in[v % RING], 16)

            def units(seg):
                L, b = seg.layer, seg.batch
                for step in UNIT_DMAS.get((seg.name, "start"), ()):
                    step(seg)
                for u in range(L.units):
                    for v in seg.loads(u):
                        held(pv_mm, tile_no(b, L, u, 0) + FREE_P)
                        if v == L.units and seg.prepare:
                            prepared(seg)
                        if v == L.units and seg.between:
                            projected(seg)
                        load_unit(*seg.unit(v))
                    if seg.has(u + 1):
                        guard_rows(seg, u + 1)
                    if L.one and seg.has(u + 2) and seg.unit(u + 2)[0] is L1:
                        held(selt_v, b * 8 + (u + 1))
                        if u + 2 == L.units:
                            held(pos_out, seg.other * 16 + 16)
                        load_positions(*seg.unit(u + 2)[1:])
                    for step in UNIT_DMAS.get((seg.name, u), ()):
                        step(seg)
                held(x_read, seg.x("scatter" if L.one else "turn", L.units - 1) + 1)
                sp.dma_start(one(att1_dram if L.one else att2_dram, b).rearrange("b p n -> (b p) n"),
                             att[:, :, :].rearrange("p t d -> p (t d)")).then_inc(att_out, 16)

            def load_xT(seg):
                sp.dma_start(xT[:, :], one(t_in["xT"], seg.other).rearrange("b d t -> (b d) t")).then_inc(xT_in, 16)

            def store_k1(seg):
                held(kp_rdy, seg.other + 1)
                for s in range(SLOTS):
                    sp.dma_start(one(k1_dram, seg.other)[:, :, s].rearrange("b d t -> (b d) t"),
                                 k_part[K_SLOTS[s]][:, :]).then_inc(k1_out, 16)

            def store_positions(seg):
                held(pos_rdy, seg.other + 1)
                sp.dma_start(one(pos_dram, seg.other).rearrange("b h t -> (b h) t"), pos_row[0:P:8, :]).then_inc(pos_out, 16)

            def prepared(seg):
                held(k1_out, seg.other * 96 + 96)
                held(x_read, seg.x("v", 1) + 1)

            def load_between(seg):
                held(att_out, att_stored(seg.other, L1) + 16)
                for dst, src in ((x_tok[:, :, :], tokens(t_in["x"], seg.other)),
                                 (att_in[:, :, :].rearrange("p t d -> p (t d)"),
                                  one(att1_dram, seg.other).rearrange("b p n -> (b p) n"))):
                    sp.dma_start(dst, src).then_inc(mid_in, 16)

            def store_x1(seg):
                held(x1_rdy, seg.other + 1)
                sp.dma_start(one(x1_dram, seg.other).rearrange("b p n -> (b p) n"),
                             x1[:, :, :].rearrange("p t d -> p (t d)")).then_inc(x1_out, 16)

            def store_q2(seg):
                held(qp_rdy, seg.other + (B + 1))
                for s in range(SLOTS):
                    sp.dma_start(one(q2_dram, seg.other)[:, :, s].rearrange("b d t -> (b d) t"),
                                 q_part[Q_SLOTS[s]][:, :]).then_inc(qk2_out, 16)

            def store_k2(seg):
                held(kp_rdy, seg.other + (B + 1))
                for s in range(SLOTS):
                    sp.dma_start(one(k2_dram, seg.other)[:, :, s].rearrange("b d t -> (b d) t"),
                                 k_part[K_SLOTS[s]][:, :]).then_inc(qk2_out, 16)

            def projected(seg):
                held(qk2_out, seg.other * 192 + 192)
                held(x1_out, seg.other * 16 + 16)
                held(x_read, seg.x("v2", 1) + 1)

            def load_finish(seg):
                held(att_out, att_stored(seg.done, L2) + 16)
                for dst, src in ((fin_in, att2_dram), (x1_in, x1_dram)):
                    sp.dma_start(dst[:, :, :].rearrange("p t d -> p (t d)"),
                                 one(src, seg.done).rearrange("b p n -> (b p) n")).then_inc(fin_in_s, 16)

            def store_output(seg):
                held(y_rdy, seg.done + 1)
                sp.dma_start(tokens(out, seg.done), y_sb[:, :, :]).then_inc(y_out, 16)

            def output_stored(seg):
                held(y_out, seg.done * 16 + 16)

            UNIT_DMAS = {("loop1", "start"): (load_xT,), ("last1", "start"): (load_between,),
                         ("head2", "start"): (load_between,), ("loop2", "start"): (load_between,),
                         ("loop2", 1): (load_finish,), ("last2", 1): (load_finish,),
                         ("loop1", 3): (store_k1,), ("loop1", 5): (store_positions,),
                         ("last1", 3): (store_x1,), ("last1", 5): (store_q2, store_k2),
                         ("head2", 5): (store_x1,), ("loop2", 5): (store_x1,),
                         ("head2", 9): (store_q2,), ("loop2", 9): (store_q2, store_output),
                         ("last2", 9): (store_output,),
                         ("head2", 10): (store_k2,), ("loop2", 10): (store_k2,),
                         ("loop2", 13): (output_stored,), ("last2", 13): (output_stored,)}

            def body(seg):
                if seg.name == "first":
                    load_xT(seg)
                    store_k1(seg)
                    store_positions(seg)
                    prepared(seg)
                    for u in range(3):
                        load_unit(*seg.unit(u))
                    held(pos_out, 16)
                    for u in range(2):
                        load_positions(*seg.unit(u)[1:])
                    guard_rows(seg, 0)
                elif seg.name == "end":
                    load_finish(seg)
                    store_output(seg)
                else:
                    units(seg)

            run(sp, body)
            sp.wait_ge(y_out, B * 16)
            sp.wait_ge(att_out, 2 * B * 16 + FREE_A)

        @block.gpsimd
        def _(pool):
            pool.memset(o2w[:, :, :], 0.0).then_inc(w_zero, 1)
            pool.memset(o2b[:, :, :], 0.0).then_inc(w_zero, 1)
            pool.memset(ident[:, :], 0.0).then_inc(c_pool, 1)
            pool.memset(same_head[:, :], 1.0).then_inc(c_pool, 1)
            pool.iota(iota_i[:, :], pattern=[[1, TOP]], base=1, channel_multiplier=0).then_inc(c_pool, 1)
            pool.iota(iota_pi[:, :], pattern=[[HALF, 2]], base=1, channel_multiplier=1).then_inc(c_pool, 1)
            pool.iota(lane[:, :], pattern=[[0, 2]], base=0, channel_multiplier=1).then_inc(c_pool, 1)
            pool.wait_ge(c_pool, 5)
            pool.affine_select(ident[:, :], ident[:, :], [[-1, P]], ALU.not_equal, 1.0, 0, 1).then_inc(c_pool, 1)
            heads = same_head[:, :].rearrange("p (g c) -> p g c", c=8)
            pool.affine_select(heads, heads, [[-8, H1], [0, 8]], ALU.is_ge, 0.0, 0, 1).then_inc(c_pool, 1)
            pool.wait_ge(c_pool, 7)
            pool.affine_select(heads, heads, [[8, H1], [0, 8]], ALU.is_ge, 0.0, 7, -1).then_inc(c_pool, 1)
            pool.wait_ge(c_rdy, 1)

            def split(no, src, part, rdy):
                n = no * 3
                pool.tensor_tensor(part[0][:, :], src[:, :], ones_t[:, :], ALU.mult).then_inc(p_step, 1)
                pool.wait_ge(p_step, n + 1)
                pool.tensor_tensor(rest[:, :], src[:, :], part[0][:, :], ALU.subtract).then_inc(p_step, 1)
                pool.wait_ge(p_step, n + 2)
                pool.tensor_tensor(part[1][:, :], rest[:, :], ones_t[:, :], ALU.mult).then_inc(p_step, 1)
                pool.wait_ge(p_step, n + 3)
                pool.tensor_tensor(part[2][:, :], rest[:, :], part[1][:, :], ALU.subtract).then_inc(rdy, 1)

            def split_q(seg):
                pool.wait_ge(x_read, seg.x("q", 1) + 1)
                split(seg.other * 2, q32, q_part, qp_rdy)

            def split_k(seg):
                pool.wait_ge(x_read, seg.x("k", 1) + 1)
                pool.wait_ge(qp_rdy, seg.other + 1)
                split(seg.other * 2 + 1, k32, k_part, kp_rdy)

            def split_q2(seg):
                pool.wait_ge(x_read, seg.x("q2", 1) + 1)
                split(seg.other * 2 + 2 * B, q32, q_part, qp_rdy)

            def split_k2(seg):
                pool.wait_ge(x_read, seg.x("k2", 1) + 1)
                pool.wait_ge(qp_rdy, seg.other + (B + 1))
                split(seg.other * 2 + (2 * B + 1), k32, k_part, kp_rdy)

            def sel_tiles(seg, u):
                n, v = seg.units, seg.unit(u)[2]
                if seg.prepare and u >= n:
                    pool.wait_ge(x_read, seg.x("position", 0) + 1)
                slot_read(pool, seg, u)
                pool.sem_inc(p_hold, 1)
                for i in range(dve_tiles(seg), 16):
                    h, t = i // TT, i % TT
                    ins = pool.tensor_scalar(sel[:, v % 2, h, t, :], iota_u[:, :], pos_col[:, t, 2 * v + h:2 * v + h + 1],
                                             None, ALU.is_equal)
                ins.then_inc(sel_p, 1)

            def deviations(no):
                pool.wait_ge(sd_rdy, no + 1)
                pool.tensor_tensor(var[:, :], mv[:, :, 1], eps_t[:, :], ALU.add).then_inc(p_var, 1)
                pool.wait_ge(p_var, no + 1)
                pool.tensor_tensor(rstd[:, :], var[:, :], power[:, :], ALU.pow).then_inc(rt_rdy, 1)

            def body(seg):
                if seg.name == "first":
                    split_q(seg)
                    split_k(seg)
                    for u in range(3):
                        sel_tiles(seg, u)
                elif seg.layer is L1:
                    for u in range(L1.units):
                        if seg.prepare and u == 1:
                            split_q(seg)
                        if seg.prepare and u == 2:
                            split_k(seg)
                        if seg.between and u in (1, 2):
                            deviations(norm_no(seg, u - 1))
                        if seg.unit(u + 3)[0] is L1:
                            sel_tiles(seg, u + 3)
                    if seg.between:
                        split_q2(seg)
                        split_k2(seg)
                else:
                    if seg.between:
                        deviations(norm_no(seg, 0))
                        deviations(norm_no(seg, 1))
                    if seg.finish:
                        deviations(norm_no(seg, 2))
                    if seg.between:
                        split_q2(seg)
                        split_k2(seg)

            run(pool, body)

        @block.scalar
        def _(act):
            def exps(seg, u, kt):
                L, n = seg.layer, tile_no(seg.batch, seg.layer, u, kt)
                act.wait_ge(score_mm, n + 1)
                act.wait_ge(pv_mm, n + (1 - RING + FREE_P))
                act.activation(probs[:, kt % RING, 0:L.nq], sbank[kt % 2][:, 0:L.nq], ACT.Exp,
                               scale=L.scale).then_inc(exp_done, 1)

            def copy_queries(seg, u):
                act.wait_ge(x_mm, seg.x("gather", u) + 1)
                v = seg.unit(u)[2]
                act.activation(queries[0:ROWS, v % RING, 0:L1.nq], xbank[0:ROWS, 0:L1.nq], ACT.Copy).then_inc(x_read, 1)

            def copy_values(seg, u):
                L = seg.layer
                act.wait_ge(pv_mm, tile_no(seg.batch, L, u, TT - 1) + (1 + FREE_P))
                act.activation(pv_sb[:, u % 2, 0:L.qw], vbank[:, 0:L.qw], ACT.Copy).then_inc(pv_ev, 1)

            def halves(dst, i):
                return dst[:, 512 * i:512 * i + 512]

            def step(seg, name, i):
                if name == "spread":
                    if i == 0:
                        act.wait_ge(qp_rdy, seg.other + 1)
                    to = q_slots[:, :, :, :].rearrange("p t (g h) (x d s) -> p (t g) h x d s", h=2, x=2, s=SLOTS)
                    frm = q_part[Q_SLOTS[i]][:, :].rearrange("p (a h d) -> p a h d", h=2, d=HD1)
                    for h in range(2):
                        act.activation(to[:, :, h, h, :, i], frm[:, :, h, :], ACT.Copy).then_inc(qs_rdy, 1)
                if name not in ("q", "k", "v", "norm", "at", "xt", "q2", "k2", "v2", "ft"):
                    return
                act.wait_ge(x_mm, seg.x(name, i) + 1)
                if name == "q":
                    ins = act.activation(halves(q32, i), xbank[:, :], ACT.Copy)
                elif name == "k":
                    ins = act.activation(halves(k32, i), xbank[:, :], ACT.Identity, bias=cols[:, 0:1])
                elif name == "v":
                    if seg.layer is not None and i == 0:
                        act.wait_ge(kv_in[3], kv_count(seg.batch, L1, 7))
                        act.wait_ge(kv_in[2], kv_count(seg.batch, L1, 6))
                        act.wait_ge(kv_in[1], kv_count(seg.batch, L1, 5))
                        act.wait_ge(kv_in[0], kv_count(seg.batch, L1, 4))
                    frm = xbank[:, :].rearrange("p (t g h d) -> p g t h d", g=PAIRS, h=2, d=HD1)
                    act.activation(v1_all[:, :, 4 * i:4 * i + 4, 0, 0:HD1], frm[:, :, :, 0, :], ACT.Copy)
                    ins = act.activation(v1_all[:, :, 4 * i:4 * i + 4, 1, 0:HD1], frm[:, :, :, 1, :], ACT.Copy)
                elif name == "norm":
                    ins = act.activation(halves(norms, i), xbank[:, :], ACT.Copy)
                elif name == "at":
                    ins = act.activation(halves(tr, i), xbank[:, :], ACT.Copy)
                elif name == "xt":
                    ins = act.activation(halves(tr, i), xbank[:, :], ACT.Identity, bias=cols[:, 4:5], scale=cols[:, 3:4])
                elif name == "q2":
                    ins = act.activation(halves(q32, i), xbank[:, :], ACT.Identity, bias=cols[:, 1:2])
                elif name == "k2":
                    ins = act.activation(halves(k32, i), xbank[:, :], ACT.Identity, bias=cols[:, 2:3])
                elif name == "v2":
                    if seg.layer is L2 and i == 0:
                        for s in range(RING):
                            act.wait_ge(kv_in[s], kv_count(seg.batch, L2, 8 + 2 * s))
                    ins = act.activation(v2_all[:, :, 4 * i:4 * i + 4, 0:HD2],
                                         xbank[:, :].rearrange("p (t h d) -> p h t d", h=H2, d=HD2), ACT.Copy)
                elif name == "ft":
                    ins = act.activation(halves(fin_tr, i), xbank[:, :], ACT.Copy)
                ins.then_inc(x_read, 1)

            def slot(seg, n):
                for name, i in seg.steps.get(n, ()):
                    step(seg, name, i)

            def body(seg):
                L = seg.layer
                if L is None:
                    for n in sorted(seg.steps):
                        slot(seg, n)
                    if seg.prepare:
                        for u in range(AHEAD):
                            copy_queries(seg, u)
                    return
                for u in range(L.units):
                    for kt in range(TT):
                        exps(seg, u, kt)
                        if kt == 0 and ("gather", u + AHEAD) in seg.index:
                            copy_queries(seg, u + AHEAD)
                        for j, at in enumerate(seg.slot_kt):
                            if kt == at:
                                slot(seg, u * seg.slots + j)
                    copy_values(seg, u)

            act.sem_inc(exp_done, FREE_S)
            act.sem_inc(pv_ev, FREE_V)
            act.wait_ge(c_rdy, 1)
            act.wait_ge(w_in, 16 * (7 + 4 + 5 + 2 * SEG))
            run(act, body)

        @block.vector
        def _(dve):
            STEPS = VECTOR_STEPS
            done = [0, 0]

            def own(seg, ins):
                done[1] += 1
                ins.then_inc(v_step, 1)
                dve.wait_ge(v_step, seg.it * STEPS[seg.name] + (done[0] + done[1]))

            dve.memset(ones_row[:, :], 1.0).then_inc(c_vec, 1)
            dve.memset(ones_t[:, :], 1.0).then_inc(c_vec, 1)
            dve.memset(eps_t[:, :], EPS).then_inc(c_vec, 1)
            dve.memset(power[:, :], -0.5).then_inc(c_vec, 1)
            dve.memset(keys[ROWS:KR, :, :], 1.0).then_inc(c_vec, 1)
            dve.memset(v1_all[:, :, :, :, :], 0.0).then_inc(c_vec, 1)
            dve.memset(v2_all[:, :, :, :], 0.0).then_inc(c_vec, 1)
            dve.wait_ge(c_vec, 7)
            dve.memset(v1_all[:, :, :, :, HD1:HD1 + 1], 1.0).then_inc(c_vec, 1)
            dve.memset(v2_all[:, :, :, HD2:HD2 + 1], 1.0).then_inc(c_vec, 1)
            dve.memset(q_slots[:, :, :, :].rearrange("p a b c -> p (a b c)").bitcast(F32), 0.0).then_inc(c_vec, 1)
            dve.wait_ge(c_pool, 8)
            dve.tensor_copy(ident_b[:, :], ident[:, :]).then_inc(c_vec, 1)
            dve.tensor_copy(iota_u[:, :], iota_i[:, :]).then_inc(c_vec, 1)
            dve.tensor_copy(iota_p[:, :], iota_pi[:, :]).then_inc(c_vec, 1)
            dve.tensor_scalar(lane[:, 1:2], lane[:, 0:1], 7, None, ALU.bitwise_and).then_inc(c_vec, 1)
            dve.wait_ge(c_vec, 14)
            for r in range(ROUNDS - 1):
                dve.tensor_scalar(digit[:, r:r + 1], lane[:, 1:2], SHIFTS[r], None, ALU.logical_shift_left).then_inc(c_vec, 1)
            dve.tensor_scalar(digit[:, ROUNDS - 1:], lane[:, 1:2], 1, None, ALU.min).then_inc(c_vec, 1)
            dve.wait_ge(c_vec, 14 + ROUNDS)
            dve.sem_inc(max_red, FREE_M)
            dve.nop().then_inc(c_rdy, 1)

            def squares(seg):
                dve.wait_ge(x_read, seg.x("q", 1) + 1)
                own(seg, dve.tensor_tensor(cum[:, :], q32[:, :], q32[:, :], ALU.mult))
                own(seg, dve.tensor_reduce(n2[:, :], cum[:, :].rearrange("p (a d) -> p a d", d=HD1), AX_X, ALU.add))
                dve.tensor_copy(n2rep[:, :, :, :].rearrange("p t h c -> p (t h) c"),
                                n2[:, :].rearrange("p (a o) -> p a o", o=1).broadcast_to([P, TT * H1, 8])).then_inc(n2_rdy, 1)

            def round_start(seg, r):
                if r == 0:
                    dve.wait_ge(x_read, seg.x("norm", 1) + 1)
                    own(seg, dve.memset(found[:, 0:1], 0))
                own(seg, dve.tensor_tensor(found[:, 1:2], found[:, 0:1], digit[:, r:r + 1], ALU.bitwise_or))
                own(seg, dve.tensor_scalar(cmp[:, :], norms[:, :], found[:, 1:2].bitcast(F32), None, ALU.is_ge,
                                           ALU.add, accum_out=count[:, 0:1]))
                dve.tensor_scalar(count_b[:, :], count[:, 0:1], TOP - 0.5, None, ALU.is_ge).then_inc(cnt_rdy, 1)

            def round_finish(seg, r):
                dve.wait_ge(x_mm, seg.x("round", r) + 1)
                dve.tensor_scalar(count[:, 1:2], xbank[:, 0:1], -1.0, float(1 << SHIFTS[r]), ALU.add, ALU.mult)\
                   .then_inc(x_read, 1)
                dve.wait_ge(x_read, seg.x("round", r) + 1)
                if r < ROUNDS - 1:
                    own(seg, dve.tensor_copy(found[:, 2:3], count[:, 1:2]))
                else:
                    own(seg, dve.tensor_scalar(found[:, 2:3], count[:, 1:2], 1.0, None, ALU.min))
                own(seg, dve.tensor_tensor(found[:, 0:1], found[:, 0:1], found[:, 2:3], ALU.bitwise_or))

            def positions(seg):
                limit = found[:, 0:1].bitcast(F32)
                own(seg, dve.tensor_scalar(cmp[:, :], norms[:, :], limit, None, ALU.is_gt, ALU.add, accum_out=count[:, 0:1]))
                own(seg, dve.tensor_scalar(count[:, 1:2], count[:, 0:1], -1.0, float(TOP), ALU.mult, ALU.add))
                own(seg, dve.tensor_scalar(norms[:, :], norms[:, :], limit, None, ALU.is_equal))
                own(seg, dve.tensor_tensor_scan(cum[:, :], ones_t[:, :], norms[:, :], 0.0, ALU.mult, ALU.add))
                own(seg, dve.scalar_tensor_tensor(norms[:, :], cum[:, :], count[:, 1:2], norms[:, :], ALU.is_le, ALU.mult))
                own(seg, dve.tensor_tensor(cmp[:, :], cmp[:, :], norms[:, :], ALU.add))
                own(seg, dve.tensor_tensor_scan(cum[:, :], ones_t[:, :], cmp[:, :], 0.0, ALU.mult, ALU.add))
                dve.tensor_tensor(pos_row[:, :], cum[:, :], cmp[:, :], ALU.mult).then_inc(pos_rdy, 1)

            def position_columns(seg):
                dve.wait_ge(x_mm, seg.x("position", 0) + 1)
                if seg.layer is not None:
                    dve.wait_ge(sel_p, seg.batch * 8 + 8)
                dve.tensor_copy(pos_col[:, :, :], xbank_b.rearrange("p (t h c) -> p t h c", t=TT, c=8)[:, :, :, 0])\
                   .then_inc(x_read, 1)
                dve.wait_ge(x_read, seg.x("position", 0) + 1)

            def build_sel(seg, u):
                v = seg.unit(u)[2]
                slot_read(dve, seg, u)
                for i in range(dve_tiles(seg)):
                    h, t = i // TT, i % TT
                    ins = dve.tensor_scalar(sel[:, v % 2, h, t, :], iota_u[:, :], pos_col[:, t, 2 * v + h:2 * v + h + 1],
                                            None, ALU.is_equal)
                ins.then_inc(sel_v, 1)

            def build_sel_t(seg, u):
                dve.wait_ge(pb_in[u % 2], seg.batch * 64 + 16 * (u // 2 + 1))
                for h in range(2):
                    for half in range(2):
                        ins = dve.tensor_scalar(sel_t[:, u % 2, h, half, :], pos_b[:, u % 2, h, :],
                                                iota_p[0:HALF, half:half + 1], None, ALU.is_equal)
                ins.then_inc(selt_v, 1)

            def maximum(seg, u, q):
                L, b, v = seg.unit(u)
                dve.wait_ge(max_mm, qt_no(b, L, v, q) + 1)
                dve.tensor_reduce(mx[0:L.qw, v % 2, q:q + 1], mbank[q % 2][0:L.qw, :], AX_X, ALU.max).then_inc(max_red, 1)

            def guard_parts(seg, u):
                L, b, v = seg.unit(u)
                w = L.qw
                dve.wait_ge(max_red, qt_no(b, L, v, QTS - 1) + (1 + FREE_M))
                g, m = g_part[0:w, v % 2], mx[0:w, v % 2, :]
                own(seg, dve.tensor_scalar(g[:, 0, :], m, -1.0, None, ALU.mult))
                own(seg, dve.scalar_tensor_tensor(mx_rest[0:w, :], m, -1.0, g[:, 0, :], ALU.mult, ALU.subtract))
                dve.tensor_copy(g[:, 1, :], mx_rest[0:w, :]).then_inc(gp_rdy, 1)

            def guard_copy(seg, u):
                L, b, v = seg.unit(u)
                dve.wait_ge(x_mm, seg.x("guard", u) + 1)
                dve.tensor_copy(g_row[:, v % RING, 0:L.qw], xbank_b[0:GUARD * QTS, 0:L.qw]).then_inc(x_read, 1)

            def norm_outputs(seg, u):
                L, w, d = seg.layer, seg.layer.qw, seg.layer.hd
                x = seg.x("turn", u) + 1
                dve.wait_ge(x_mm, x)
                turned = xbank[0:w, 0:P].rearrange("p (g r) -> p g r", r=VW)
                own(seg, dve.reciprocal(den[0:w, :], turned[:, :, d]))
                share = den[0:w, :].rearrange("p (g o) -> p g o", o=1).broadcast_to([w, QTS, d])
                if not L.one:
                    t0, c0 = QTS * (u % 2), HD2 * (u // 2)
                    if u == 0:
                        dve.wait_ge(att_out, att_stored(seg.batch, L2))
                    dve.tensor_tensor(att[:, t0:t0 + QTS, c0:c0 + HD2], turned[:, :, 0:d], share, ALU.mult).then_inc(x_read, 1)
                    return
                dve.tensor_tensor(o_sel[:, :, :], turned[:, :, 0:d], share, ALU.mult).then_inc(x_read, 1)
                dve.wait_ge(x_read, x)
                parts = o_part[:, u % 2]
                own(seg, dve.tensor_copy(parts[:, :, 0, :], o_sel[:, :, :]))
                own(seg, dve.tensor_tensor(o_rest[:, :, :], o_sel[:, :, :], parts[:, :, 0, :], ALU.subtract))
                own(seg, dve.tensor_copy(parts[:, :, 1, :], o_rest[:, :, :]))
                dve.tensor_tensor(parts[:, :, 2, :], o_rest[:, :, :], parts[:, :, 1, :], ALU.subtract).then_inc(on_rdy, 1)

            def sum_scattered(seg, u):
                dve.wait_ge(x_mm, seg.x("scatter", u) + 1)
                if u == 0:
                    dve.wait_ge(att_out, att_stored(seg.batch, L1))
                x = xbank[:, 0:TT * 2 * 3 * HD1].rearrange("p (t h s d) -> p t h d s", t=TT, h=2, s=3)
                dve.tensor_reduce(att[:, :, 16 * u:16 * u + 8], x[:, :, 0], AX_X, ALU.add)
                dve.tensor_reduce(att[:, :, 16 * u + 8:16 * u + 16], x[:, :, 1], AX_X, ALU.add).then_inc(x_read, 1)

            def statistics(seg, src):
                for t in range(TT):
                    ins = dve.bn_stats(stats[:, t, :], src[:, t, :])
                own(seg, ins)
                dve.sem_inc(v_hold, 1)
                for t in range(TT):
                    ins = dve.bn_aggr(mv[:, t, :], stats[:, t, :])
                ins.then_inc(sd_rdy, 1)

            def normalise(no, src, dst, rdy):
                dve.wait_ge(rt_rdy, no + 1)
                for t in range(TT):
                    ins = dve.tensor_scalar(dst[:, t, :], src[:, t, :], mv[:, t, 0:1], rstd[:, t:t + 1],
                                            ALU.subtract, ALU.mult)
                ins.then_inc(rdy, 1)

            def start(seg, name, i):
                if name == "squares":
                    squares(seg)
                elif name == "round":
                    round_start(seg, i)
                elif name == "positions":
                    positions(seg)
                elif name == "norm1":
                    statistics(seg, zt)
                elif name == "norm2":
                    normalise(norm_no(seg, 0), zt, x1, x1_rdy)
                    dve.wait_ge(x1_rdy, seg.other + 1)
                    statistics(seg, x1)
                elif name == "norm3":
                    normalise(norm_no(seg, 1), x1, xh, xh_rdy)
                elif name == "norm4":
                    statistics(seg, fin_in)
                elif name == "norm5":
                    normalise(norm_no(seg, 2), fin_in, y_sb, y_rdy)

            def finish(seg, name, i):
                t0 = 4 * i
                if name == "round":
                    round_finish(seg, i)
                elif name == "position":
                    position_columns(seg)
                elif name == "y":
                    dve.wait_ge(mid_in, seg.other * 32 + 32)
                    dve.wait_ge(x_mm, seg.x("y", i) + 1)
                    dve.tensor_tensor(zt[:, t0:t0 + 4, :].rearrange("p t d -> p (t d)"), xbank[:, :],
                                      x_tok[:, t0:t0 + 4, :].rearrange("p t d -> p (t d)"), ALU.add).then_inc(x_read, 1)
                    dve.wait_ge(x_read, seg.x("y", i) + 1)
                elif name == "fo":
                    dve.wait_ge(fin_in_s, seg.done * 32 + 32)
                    dve.wait_ge(x_mm, seg.x("fo", i) + 1)
                    dve.scalar_tensor_tensor(fin_in[:, t0:t0 + 4, :].rearrange("p t d -> p (t d)"),
                                             x1_in[:, t0:t0 + 4, :].rearrange("p t d -> p (t d)"), 2.0, xbank[:, :],
                                             ALU.mult, ALU.add).then_inc(x_read, 1)
                    dve.wait_ge(x_read, seg.x("fo", i) + 1)

            def slot(seg, n, between=()):
                for name, i in seg.steps.get(n, ()):
                    start(seg, name, i)
                for work in between:
                    work()
                for name, i in seg.steps.get(n, ()):
                    finish(seg, name, i)

            def first_units(seg):
                for n in sorted(seg.steps):
                    slot(seg, n)
                for u in range(3):
                    build_sel(seg, u)
                for q in range(QTS):
                    maximum(seg, 0, q)
                guard_parts(seg, 0)
                guard_copy(seg, 0)
                for q in range(QTS):
                    maximum(seg, 1, q)

            def first_layer(seg):
                n = L1.units
                for u in range(n):
                    guard_parts(seg, u + 1)
                    slot(seg, u * 4, [lambda: build_sel(seg, u + 3)] if seg.unit(u + 3)[0] is L1 else [])
                    guard_copy(seg, u + 1)
                    if u > 0:
                        norm_outputs(seg, u - 1)
                    maximum(seg, u + AHEAD, 0)
                    slot(seg, u * 4 + 1, [lambda: build_sel_t(seg, u), lambda: maximum(seg, u + AHEAD, 1)])
                    if u > 0:
                        sum_scattered(seg, u - 1)
                    slot(seg, u * 4 + 2, [lambda: maximum(seg, u + AHEAD, 2)])
                    slot(seg, u * 4 + 3, [lambda: maximum(seg, u + AHEAD, 3)])
                norm_outputs(seg, n - 1)
                sum_scattered(seg, n - 1)

            def second_layer(seg):
                n = L2.units
                for u in range(n):
                    ahead = seg.has(u + AHEAD)
                    if seg.has(u + 1):
                        guard_parts(seg, u + 1)
                    if ahead:
                        maximum(seg, u + AHEAD, 0)
                    slot(seg, 2 * u)
                    if seg.has(u + 1):
                        guard_copy(seg, u + 1)
                    if ahead:
                        maximum(seg, u + AHEAD, 1)
                    if u > 0:
                        norm_outputs(seg, u - 1)
                    if ahead:
                        maximum(seg, u + AHEAD, 2)
                    slot(seg, 2 * u + 1, [lambda: maximum(seg, u + AHEAD, 3)] if ahead else [])
                norm_outputs(seg, n - 1)

            def body(seg):
                if seg.layer is L1:
                    first_layer(seg)
                elif seg.layer is L2:
                    second_layer(seg)
                elif seg.prepare:
                    first_units(seg)
                else:
                    for n in sorted(seg.steps):
                        slot(seg, n)
                assert done[1] == STEPS[seg.name], (seg.name, done[1])
                done[0] += done[1] * seg.times
                done[1] = 0

            run(dve, body)

        @block.tensor
        def _(pe):
            def with_row(dst, lhsT, rhs, bias):
                pe.matmul(dst, lhsT, rhs, start=True, stop=False)
                return pe.matmul(dst, ones_row[:, :], bias, start=False, stop=True)

            def tile(bank, t, w=P):
                return bank[:, t * w:t * w + w]

            def small_bank(seg, *key):
                if seg.before + seg.index[key]:
                    pe.wait_ge(x_read, seg.x(*key))

            def gather(seg, u):
                small_bank(seg, "gather", u)
                _, b, v = seg.unit(u)
                if v == 0:
                    pe.wait_ge(qs_rdy, b * 12 + 12)
                pe.wait_ge(sel_v, b * 8 + (v + 1))
                pe.wait_ge(sel_p, b * 8 + (v + 1))
                for h in range(2):
                    for t in range(TT):
                        ins = pe.matmul(xbank[0:ROWS, h * TOP:h * TOP + TOP], q_slots[:, t, 2 * v + h, :],
                                        sel[:, v % 2, h, t, :], start=(t == 0), stop=(t == TT - 1))
                ins.then_inc(x_mm, 1)

            def max_scores(seg, u, q, halves=(0, 1)):
                L, b, v = seg.unit(u)
                i, s = qt_no(b, L, v, q), L.slot(v)
                if 0 in halves:
                    if q == 0:
                        pe.wait_ge(kv_in[s], kv_count(b, L, v))
                        if L.one:
                            pe.wait_ge(x_read, seg.x("gather", u) + 1)
                    pe.wait_ge(max_red, i + (1 - 2 + FREE_M))
                c0 = L.q0(v) + q * L.qw
                for c in halves:
                    ins = pe.matmul(mbank[q % 2][0:L.qw, c * 512:c * 512 + 512], queries[0:ROWS, s, c0:c0 + L.qw],
                                    keys[0:ROWS, s, c * 512:c * 512 + 512], start=True, stop=True)
                if 1 in halves:
                    ins.then_inc(max_mm, 1)

            def turn_guard(seg, u):
                L, b, v = seg.unit(u)
                w = L.qw
                small_bank(seg, "guard", u)
                pe.wait_ge(gp_rdy, unit_no(b, L, v) + 1)
                pe.transpose(xbank_b[0:GUARD * QTS, 0:w], g_part[0:w, v % 2].rearrange("p a b -> p (a b)"),
                             ident_b[0:w, 0:w]).then_inc(x_mm, 1)

            def scores(seg, u, kt):
                L, b = seg.layer, seg.batch
                s, q0 = L.slot(u), L.q0(u)
                if kt == 0:
                    pe.wait_ge(guard_in[u % RING], guard_count(b, L, u))
                pe.wait_ge(exp_done, tile_no(b, L, u, kt) + (1 - 2 + FREE_S))
                pe.matmul(sbank[kt % 2][:, 0:L.nq], keys[:, s, kt * P:kt * P + P],
                          queries[:, s, q0:q0 + L.nq], start=True, stop=True).then_inc(score_mm, 1)

            def add_values(seg, u, kt):
                L, b = seg.layer, seg.batch
                pe.wait_ge(exp_done, tile_no(b, L, u, kt) + (1 + FREE_S))
                if kt == 0:
                    pe.wait_ge(pv_ev, unit_no(b, L, u) + FREE_V)
                s, w = L.slot(u), L.qw
                for g in range(QTS):
                    c = (kt * 2 + g // 2) * VW if L.one else kt * VW
                    ins = pe.matmul(vbank[VW * g:VW * g + VW, 0:w], values[:, s, c:c + VW],
                                    probs[:, kt % RING, g * w:g * w + w], start=(kt == 0), stop=(kt == TT - 1))
                ins.then_inc(pv_mm, 1)

            def turn_outputs(seg, u):
                L, w = seg.layer, seg.layer.qw
                small_bank(seg, "turn", u)
                pe.wait_ge(pv_ev, unit_no(seg.batch, L, u) + (1 + FREE_V))
                pe.transpose(xbank[0:w, 0:P], pv_sb[:, u % 2, 0:w], ident[:, :]).then_inc(x_mm, 1)

            def scatter(seg, u):
                small_bank(seg, "scatter", u)
                pe.wait_ge(on_rdy, seg.batch * 8 + (u + 1))
                pe.wait_ge(selt_v, seg.batch * 8 + (u + 1))
                for t in range(TT):
                    for h in range(2):
                        c = (t * 2 + h) * 3 * HD1
                        for half in range(2):
                            ins = pe.matmul(xbank[:, c:c + 3 * HD1], sel_t[:, u % 2, h, half, t * P:t * P + P],
                                            o_part[:, u % 2, 2 * h + half].rearrange("p s d -> p (s d)"),
                                            start=(half == 0), stop=(half == 1))
                ins.then_inc(x_mm, 1)

            def step(seg, name, i):
                if name not in BANK_STEPS:
                    return
                small_bank(seg, name, i)
                four = range(4 * i, 4 * i + 4)
                if name == "q":
                    if i == 0:
                        pe.wait_ge(xT_in, seg.other * 16 + 16)
                    for t in four:
                        ins = with_row(tile(xbank, t % 4), tile(xT, t), wqT[:, :], rows[:, 0, :])
                elif name == "k":
                    ins = pe.matmul(xbank[:, :], wkT[:, :], tile(xT, i, 512), start=True, stop=True)
                elif name == "v":
                    for t in four:
                        ins = with_row(tile(xbank, t % 4), tile(xT, t), wvT[:, :], rows[:, 1, :])
                elif name == "norm":
                    pe.wait_ge(n2_rdy, seg.other + 1)
                    for t in four:
                        ins = pe.transpose(tile(xbank, t % 4), n2rep[:, t].rearrange("p h c -> p (h c)"), ident[:, :])
                elif name == "round":
                    pe.wait_ge(cnt_rdy, seg.other * ROUNDS + (i + 1))
                    ins = pe.matmul(xbank[:, 0:1], same_head[:, :], count_b[:, :], start=True, stop=True)
                elif name == "position":
                    pe.wait_ge(pos_rdy, seg.other + 1)
                    for t in range(TT):
                        ins = pe.transpose(tile(xbank_b, t), tile(pos_row, t), ident_b[:, :])
                elif name == "at":
                    if i == 0:
                        pe.wait_ge(mid_in, seg.other * 32 + 32)
                    for t in four:
                        ins = pe.transpose(tile(xbank, t % 4), att_in[:, t, :], ident[:, :])
                elif name == "y":
                    for t in four:
                        ins = with_row(tile(xbank, t % 4), tile(tr, t), woT[:, :], rows[:, 2, :])
                elif name == "xt":
                    pe.wait_ge(xh_rdy, seg.other + 1)
                    for t in four:
                        ins = pe.transpose(tile(xbank, t % 4), xh[:, t, :], ident[:, :])
                elif name in ("q2", "k2"):
                    w = q2w if name == "q2" else k2w
                    for e in (2 * i, 2 * i + 1):
                        m, c = D >> e, T // SEG
                        ins = pe.matmul(tile(xbank, e % 2, c), w[0:m, :], tr[0:m, e * c:e * c + c], start=True, stop=True)
                elif name == "v2":
                    for t in four:
                        m = D >> (t * SEG // TT)
                        ins = with_row(tile(xbank, t % 4), tr[0:m, t * P:t * P + P], v2w[0:m, :], rows[:, 3, :])
                elif name == "ft":
                    if i == 0:
                        pe.wait_ge(fin_in_s, seg.done * 32 + 32)
                    for t in four:
                        ins = pe.transpose(tile(xbank, t % 4), fin_in[:, t, :], ident[:, :])
                elif name == "fo":
                    for t in four:
                        e = t * SEG // TT
                        m = D >> e
                        ins = with_row(tile(xbank, t % 4), fin_tr[0:m, t * P:t * P + P], o2w[0:m, e, :], o2b[:, e, :])
                ins.then_inc(x_mm, 1)

            def slot(seg, n):
                for name, i in seg.steps.get(n, ()):
                    step(seg, name, i)

            def first_units(seg):
                for u in range(AHEAD):
                    gather(seg, u)
                for q in range(QTS):
                    max_scores(seg, 0, q)
                turn_guard(seg, 0)
                for q in range(QTS):
                    max_scores(seg, 1, q)

            def first_layer(seg):
                n = L1.units
                for u in range(n):
                    for kt in range(TT):
                        scores(seg, u, kt)
                        if kt:
                            add_values(seg, u, kt - 1)
                        if kt == 0 and ("gather", u + AHEAD) in seg.index:
                            gather(seg, u + AHEAD)
                        if kt == 2:
                            turn_guard(seg, u + 1)
                        if kt == 3 and u:
                            turn_outputs(seg, u - 1)
                        if kt in (3, 4, 5, 7):
                            max_scores(seg, u + AHEAD, (3, 4, 5, 7).index(kt))
                        if kt == 5 and u:
                            scatter(seg, u - 1)
                        for j, at in enumerate(seg.slot_kt):
                            if kt == at:
                                slot(seg, u * seg.slots + j)
                    add_values(seg, u, TT - 1)
                turn_outputs(seg, n - 1)
                scatter(seg, n - 1)

            def second_layer(seg):
                n = L2.units
                for u in range(n):
                    for kt in range(TT):
                        scores(seg, u, kt)
                        if kt:
                            add_values(seg, u, kt - 1)
                        if seg.has(u + AHEAD):
                            max_scores(seg, u + AHEAD, kt // 2, (kt % 2,))
                        if kt == 2 and seg.has(u + 1):
                            turn_guard(seg, u + 1)
                        if kt == 4 and u:
                            turn_outputs(seg, u - 1)
                        for j, at in enumerate(seg.slot_kt):
                            if kt == at:
                                slot(seg, u * seg.slots + j)
                    add_values(seg, u, TT - 1)
                turn_outputs(seg, n - 1)

            def body(seg):
                if seg.layer is L1:
                    first_layer(seg)
                elif seg.layer is L2:
                    second_layer(seg)
                else:
                    for n in sorted(seg.steps):
                        slot(seg, n)
                    if seg.prepare:
                        first_units(seg)

            pe.sem_inc(pv_mm, FREE_P)
            pe.wait_ge(c_rdy, 1)
            pe.wait_ge(w_in, 16 * (7 + 4 + 5 + 2 * SEG))
            run(pe, body)


_TURNED = {"WqT": "L0_attn_Wq", "WkT": "L0_attn_Wk", "WvT": "L0_attn_Wv", "WoT": "L0_attn_Wo",
           "q_wT": "L0_ffn_q_w", "k_wT": "L0_ffn_k_w", "v_wT": "L0_ffn_v_w", "o_wT": "L0_ffn_o_w"}
_ROWS = {"bq": "L0_attn_bq", "bv": "L0_attn_bv", "bo": "L0_attn_bo", "v_b": "L0_ffn_v_b", "o_b": "L0_ffn_o_b"}
_COLS = {"bk": "L0_attn_bk", "q_b": "L0_ffn_q_b", "k_b": "L0_ffn_k_b", "norm_w": "L0_ffn_norm_w",
         "norm_b": "L0_ffn_norm_b"}


def kernel(**inputs):
    import numpy as _np
    import concourse.bacc as _bacc
    from concourse.bass_utils import run_bass_kernel_spmd as _run

    nc = _bacc.Bacc("TRN2", target_bir_lowering=False, num_devices=1)
    x = _np.asarray(inputs["L0_attn_x"])
    given = {"x": x, "xT": x.transpose(0, 2, 1)}
    given |= {k: _np.asarray(inputs[n]).T for k, n in _TURNED.items()}
    given |= {k: _np.asarray(inputs[n]).reshape(1, D) for k, n in _ROWS.items()}
    given |= {k: _np.asarray(inputs[n]).reshape(D, 1) for k, n in _COLS.items()}
    arrays, t_in = {}, {}
    for name, a in given.items():
        a = _np.ascontiguousarray(a)
        arrays[f"in_{name}"] = a
        t_in[name] = nc.dram_tensor(f"in_{name}", a.shape, F32, kind="ExternalInput").ap()
    out = nc.dram_tensor("out", (B, T, D), F32, kind="ExternalOutput").ap()
    build(nc, t_in, out)
    r = _run(nc, [arrays], core_ids=[0])
    return r.results[0]["out"]
```

```python
from contextlib import ExitStack

import concourse.bass as bass
from concourse import mybir

ALU = mybir.AluOpType
ACT = mybir.ActivationFunctionType
AX_X = mybir.AxisListType.X
F32 = mybir.dt.float32
BF16 = mybir.dt.bfloat16
I32 = mybir.dt.int32

P = 128
B = 4
T = 1024
D = 128
TT = T // P
EPS = 1e-5

H1 = 16
HD1 = D // H1
TOP = T // 5
HALF = TOP // 2
PAIRS = H1 // 2

H2 = 8
HD2 = D // H2
SEG = 4

K_SLOTS = (0, 1, 0, 1, 2, 0)
Q_SLOTS = (0, 0, 1, 1, 0, 2)
SLOTS = len(K_SLOTS)
ROWS = 16 * SLOTS
GUARD = 2
KR = ROWS + GUARD
VW = 32

QTS = 4
RING = 4
M_BANKS = 3
AHEAD = 2

SHIFTS = tuple(range(28, 0, -3)) + (0,)
ROUNDS = len(SHIFTS)


class Layer:

    def __init__(self, index):
        self.one = index == 1
        self.units = PAIRS if self.one else 2 * H2
        self.u0 = 0 if self.one else PAIRS
        self.qw = HALF if self.one else P
        self.nq = QTS * self.qw
        self.scale = HD1 ** -0.5 if self.one else D ** -0.5
        self.hd = HD1 if self.one else HD2

    def slot(self, u):
        return (u if self.one else u // 2) % RING

    def q0(self, u):
        return 0 if self.one else u % 2 * self.nq


L1, L2 = Layer(1), Layer(2)

BANK_STEPS = {"q", "k", "v", "norm", "round", "position", "at", "y", "xt", "q2", "k2", "v2", "ft", "fo"}

PREPARE = ([(1, "q", 0), (2, "q", 1), (3, "squares", 0), (3, "k", 0), (4, "k", 1), (4, "norm", 0), (5, "norm", 1),
            (5, "upper", 0)]
           + [(6 + r, "round", r) for r in range(ROUNDS)]
           + [(17, "positions", 0), (18, "positions", 1), (19, "positions", 2), (19, "positions", 3)]
           + [(17, "v", 0), (18, "v", 1), (20, "position", 0)]
           + [(21 + s // 2, "spread", s) for s in range(SLOTS)])
PREPARE_FIRST = [({"spread": 8, "v": 6}.get(step, slot), step, i) for slot, step, i in PREPARE]
BETWEEN_1 = [(2, "at", 0), (3, "at", 1), (4, "y", 0), (5, "y", 1), (6, "norm1", 0), (9, "norm2", 0), (10, "stats2", 0), (12, "norm3", 0),
             (13, "xt", 0), (14, "xt", 1), (15, "q2", 0), (16, "q2", 1), (17, "k2", 0), (18, "k2", 1),
             (19, "split_k2", 0), (19, "v2", 0), (20, "v2", 1)]
BETWEEN_2 = [(2, "at", 0), (3, "at", 1), (4, "y", 0), (5, "y", 1), (6, "norm1", 0), (7, "norm2", 0), (8, "stats2", 0), (10, "norm3", 0),
             (11, "xt", 0), (12, "xt", 1), (13, "q2", 0), (14, "q2", 1), (15, "k2", 0), (16, "k2", 1),
             (21, "v2", 0), (22, "v2", 1)]
FINISH = [(7, "ft", 0), (8, "ft", 1), (9, "fo", 0), (10, "fo", 1), (12, "norm4", 0), (14, "norm5", 0)]

SEL_VECTOR = (14, 7, 7, 7, 8, 8, 8, 9)
COPIED = (1, 3)
VECTOR_STEPS = {"first": 45, "loop1": 83, "last1": 45, "head2": 50, "loop2": 51, "last2": 47, "end": 1}


class Segment:

    def __init__(self, name, before, times, layer=None, after=None, prepare=False, between=False, finish=False):
        self.name, self.layer, self.next_layer = name, layer, after
        self.prepare, self.between, self.finish = prepare, between, finish
        self.units = n = layer.units if layer else 0
        self.slot_kt = (1, 3, 5, 7) if layer is L1 else (1, 5)
        self.slots = len(self.slot_kt)
        self.steps = {}
        for on, todo in ((prepare, PREPARE if layer else PREPARE_FIRST), (between, BETWEEN_1 if layer is L1 else BETWEEN_2), (finish, FINISH)):
            for slot, step, i in todo if on else ():
                self.steps.setdefault(slot, []).append((step, i))
        order = []
        if layer is None:
            order += [x for slot in sorted(self.steps) for x in self.steps[slot]]
            order += [("gather", 0), ("gather", 1), ("guard", 0)] if after else []
        for u in range(n):
            at = [self.steps.get(u * self.slots + j, []) for j in range(self.slots)]
            guard = [("guard", u + 1)] if self.has(u + 1) else []
            turn = [("turn", u - 1)] if u else []
            if layer.one:
                if u + AHEAD < n or after is L1:
                    order += [("gather", u + AHEAD)]
                order += at[0] + turn + guard + at[1] + ([("scatter", u - 1)] if u else []) + at[2] + at[3]
            else:
                order += at[0] + guard + turn + at[1]
        if layer:
            order += [("turn", n - 1)] + ([("scatter", n - 1)] if layer.one else [])
        uses = [x for x in order if x[0] in ("gather", "guard", "turn", "scatter")]
        self.index = {key: i for i, key in enumerate(uses)}
        steps = [x for x in order if x[0] in BANK_STEPS]
        self.step_index = {key: i for i, key in enumerate(steps)}
        self.uses, self.step_uses, self.times = len(uses), len(steps), times
        self.before_x, self.before_y = before
        self.after = self.before_x + times * len(uses), self.before_y + times * len(steps)

    def has(self, u):
        return u < self.units or self.next_layer is not None

    def layer_of(self, u):
        return self.layer if u < self.units else self.next_layer

    def unit(self, u):
        if u < self.units:
            return self.layer, self.batch, u
        if self.next_layer is self.layer:
            return self.layer, self.batch + 1, u - self.units
        return self.next_layer, 0, u - self.units

    def loads(self, u):
        n = self.units
        if self.layer.one:
            if u + 3 < n or self.next_layer is L1:
                return [u + 3]
            return [n + 2 * (u - 6)] if u >= 6 else []
        return [u + 4] if u % 2 == 0 and self.has(u + 4) else []

    def x0(self):
        return self.it * self.uses + self.before_x

    def at(self, it, batch, other=None, done=None):
        self.it, self.batch, self.other, self.done = it, batch, other, done
        return self

    def x(self, *key):
        return self.it * self.uses + (self.before_x + self.index[key])

    def y(self, *key):
        return self.it * self.step_uses + (self.before_y + self.step_index[key])


def segments():
    plan = [("first", 1, {"after": L1, "prepare": True}),
            ("loop1", B - 1, {"layer": L1, "after": L1, "prepare": True}),
            ("last1", 1, {"layer": L1, "after": L2, "between": True}),
            ("head2", 1, {"layer": L2, "after": L2, "between": True}),
            ("loop2", B - 2, {"layer": L2, "after": L2, "between": True, "finish": True}),
            ("last2", 1, {"layer": L2, "finish": True}),
            ("end", 1, {"finish": True})]
    out, before = [], (0, 0)
    for name, times, what in plan:
        out.append(Segment(name, before, times, **what))
        before = out[-1].after
    return out


def run(engine, body):
    first, loop1, last1, head2, loop2, last2, end = segments()
    body(first.at(0, None, 0))
    with engine.Fori(0, B - 1) as i:
        body(loop1.at(i, i, i + 1))
    body(last1.at(0, B - 1, 0))
    body(head2.at(0, 0, 1))
    with engine.Fori(0, B - 2) as i:
        body(loop2.at(i, i + 1, i + 2, i))
    body(last2.at(0, B - 1, None, B - 2))
    body(end.at(0, None, None, B - 1))


def build(nc, t_in, out):
    ctx = ExitStack()
    with ctx:
        def sb(name, shape, dt=F32):
            return ctx.enter_context(nc.sbuf_tensor(name, shape, dt))

        def ps(name, shape, dt=F32):
            return ctx.enter_context(nc.psum_tensor(name, shape, dt))

        def sem(name):
            return ctx.enter_context(nc.semaphore(name))

        def dram(name, shape, dt):
            return nc.dram_tensor(name, shape, dt, kind="Internal").ap()

        k1_dram = dram("k1_parts", (B, D, SLOTS, T), BF16)
        k2_dram = dram("k2_parts", (B, D, SLOTS, T), BF16)
        q2_dram = dram("q2_parts", (B, D, SLOTS, T), BF16)
        pos_dram = dram("positions", (B, H1, T), BF16)
        att1_dram = dram("attention1", (B, P, TT * D), F32)
        att2_dram = dram("attention2", (B, P, TT * D), F32)
        x1_dram = dram("x1_tokens", (B, P, TT * D), F32)

        wqT, wkT, wvT, woT = (sb(n, [P, D]) for n in ("wqT", "wkT", "wvT", "woT"))
        q2w, k2w, v2w = (sb(n, [P, D]) for n in ("q2w", "k2w", "v2w"))
        o2w = sb("o2w", [P, SEG, D])
        rows = sb("rows", [1, 4, D])
        o2b = sb("o2b", [1, SEG, D])
        cols = sb("cols", [P, 5])
        ones_row = sb("ones_row", [1, P])
        ident = sb("ident", [P, P])
        ident_b = sb("ident_b", [P, P], BF16)
        same_head = sb("same_head", [P, P], BF16)
        iota_u = sb("iota_u", [P, TOP], BF16)
        iota_i = sb("iota_i", [P, TOP], I32)
        iota_p = sb("iota_p", [P, 2])
        iota_pi = sb("iota_pi", [P, 2], I32)
        lane = sb("lane", [P, 2], I32)
        digit = sb("digit", [P, ROUNDS], I32)
        ones_t = sb("ones_t", [P, T])

        xT = sb("xT", [P, T])
        x_tok = sb("x_tok", [P, TT, D])
        q32 = sb("q32", [P, T])
        k32 = sb("k32", [P, T])
        n2 = sb("n2", [P, TT * H1])
        norms = sb("norms", [P, T])
        cmp = sb("cmp", [P, T])
        cum = sb("cum", [P, T])
        norms16 = sb("norms16", [P, T], BF16)
        reach16 = cmp[:, 0:T // 2].bitcast(BF16)
        n2rep = cmp[:, :].rearrange("p (t h c) -> p t h c", t=TT, c=8)
        pos_row = sb("pos_row", [P, T], BF16)
        pos_col = sb("pos_col", [P, TT, H1])
        found = sb("found", [P, 3], I32)
        count = sb("count", [P, 2])
        count_b = sb("count_b", [P, 1], BF16)
        rest = sb("rest", [P, T])
        k_part = [sb(f"k_part{i}", [P, T], BF16) for i in range(3)]
        q_part = [sb(f"q_part{i}", [P, T], BF16) for i in range(3)]
        q_slots = sb("q_slots", [P, TT, H1, ROWS], BF16)
        v1_all = sb("v1_all", [P, PAIRS, TT, 2, VW])
        v2_all = sb("v2_all", [P, H2, TT, VW])
        att = sb("att", [P, TT, D])
        x1 = sb("x1", [P, TT, D])
        tr = sb("tr", [P, T])
        att_in = sb("att_in", [P, TT, D])
        fin_in = sb("fin_in", [P, TT, D])
        x1_in = norms[:, :].rearrange("p (t d) -> p t d", t=TT)
        fin_tr = xT
        zt, xh, y_sb = x_tok, att_in, fin_in
        stats = sb("stats", [P, TT, 6])
        mv = sb("mv", [P, TT, 2])
        var = sb("var", [P, TT])
        rstd = sb("rstd", [P, TT])
        eps_t = sb("eps_t", [P, TT])
        power = sb("power", [P, TT])

        keys = sb("keys", [KR, RING, T], BF16)
        queries = sb("queries", [KR, RING, T], BF16)
        values = sb("values", [P, RING, TT * 2 * VW])
        sel = sb("sel", [P, 2, 2, TT, TOP], BF16)
        sel_t = sb("sel_t", [HALF, 2, 2, 2, T], BF16)
        pos_b = sb("pos_b", [HALF, 2, 2, T], BF16)
        probs = sb("probs", [P, RING, 512])
        max_sb = sb("max_sb", [P, 2, 512], BF16)
        mx2 = sb("mx_halves", [P, 2, QTS, 2])
        mx = sb("mx", [P, QTS])
        g_part = sb("g_part", [P, 2, GUARD, QTS], BF16)
        g_row = sb("g_row", [GUARD * QTS, RING, P], BF16)
        pv_sb = sb("pv_sb", [P, 2, P])
        den = sb("den", [P, QTS])
        o_sel = sb("o_sel", [HALF, QTS, HD1])
        o_rest = sb("o_rest", [HALF, QTS, HD1])
        o_part = sb("o_part", [HALF, 2, QTS, 3, HD1], BF16)

        mbank = [ps(f"mbank{i}", [P, 512]) for i in range(M_BANKS)]
        sbank = [ps(f"sbank{i}", [P, 512]) for i in range(2)]
        vbank = ps("vbank", [P, 512])
        xbank = ps("xbank", [P, 512])
        ybank = ps("ybank", [P, 512])
        xbank_b, ybank_b = xbank[:, :].bitcast(BF16), ybank[:, :].bitcast(BF16)

        w1_in = sem("first_weights_loaded")
        w_in, w_zero = sem("weights_loaded"), sem("weights_zeroed")
        c_pool, c_vec, c_rdy = sem("constants_pool"), sem("constants_vector"), sem("constants_ready")
        c_wide = sem("wide_constants")
        xT_in, mid_in, fin_in_s = sem("xT_loaded"), sem("between_loaded"), sem("finish_loaded")
        n2_rdy, cnt_rdy, pos_rdy = sem("norms_ready"), sem("count_ready"), sem("positions_ready")
        pos_out, n16_rdy = sem("positions_stored"), sem("upper_bits_ready")
        qp_rdy, kp_rdy, qs_rdy = sem("q_parts_ready"), sem("k_parts_ready"), sem("q_slots_ready")
        k1_out, qk2_out = sem("k1_parts_stored"), sem("second_parts_stored")
        p_step, v_step = sem("pool_step"), sem("vector_step")
        kv_in = [sem(f"unit_loaded{i}") for i in range(RING)]
        pb_in = [sem(f"position_rows_loaded{i}") for i in range(2)]
        sel_v, sel_p, selt_v = sem("sel_vector"), sem("sel_pool"), sem("sel_t_ready")
        max_mm, max_red = sem("max_scores"), sem("max_reduced")
        max_cp, copy_red = sem("max_copied"), sem("max_copy_reduced")
        gp_rdy, on_rdy = sem("guard_parts"), sem("outputs_normed")
        x_mm, x_read = sem("unit_bank_written"), sem("unit_bank_read")
        y_mm, y_read = sem("step_bank_written"), sem("step_bank_read")
        guard_in = [sem(f"guard_rows_loaded{i}") for i in range(RING)]
        score_mm, exp_done, pv_mm, pv_ev = sem("scores"), sem("exponentials"), sem("values_added"), sem("values_copied")
        att_out, p_var = sem("attention_stored"), sem("variance_eps")
        x1_rdy, x1_out, xh_rdy = sem("x1_ready"), sem("x1_stored"), sem("x_hat_ready")
        sd_rdy, rt_rdy = sem("variance_ready"), sem("deviation_ready")
        y_rdy, y_out = sem("output_ready"), sem("output_stored")
        p_hold, v_hold, s_hold = sem("pool_hold"), sem("vector_hold"), sem("dma_hold")

        FREE_S, FREE_C, FREE_P, FREE_V, FREE_A = 2, 2, RING, 1, 16

        W_DMAS = 16 * (4 + 2 + 4 + 2 * SEG)

        def unit_no(b, L, u):
            return b * 8 + u if L.one else b * 16 + (B * 8 + u)

        def tile_no(b, L, u, kt):
            return b * (8 * TT) + (u * TT + kt) if L.one else b * (16 * TT) + ((B * 8 + u) * TT + kt)

        def half_no(b, L, u, q, c):
            h = 2 * q + c
            return b * (8 * 2 * QTS) + (u * 2 * QTS + h) if L.one else \
                b * (16 * 2 * QTS) + ((B * 8 + u) * 2 * QTS + h)

        def finish_loads(seg):
            return 32 * (B - 1) + 16 if seg.name == "end" else seg.done * 32 + 32

        def copied(L, q):
            return L.one and q in COPIED

        def freed(b, L, u, q, c):
            mine = [p for p in range(QTS) if copied(L1, p) == copied(L, q)]
            if L.one:
                n = 2 * len(mine)
                return b * (8 * n) + (u * n + 2 * mine.index(q) + c + 1)
            return b * 128 + (B * 16 * len(mine) + u * 8 + 2 * q + c + 1)

        def kv_count(b, L, u):
            return b * 64 + 32 * (u // RING + 1) if L.one else b * 96 + (B * 64 + 48 * (u // 2 // RING + 1))

        def guard_count(b, L, u):
            return b * 64 + 32 * (u // RING + 1) if L.one else b * 128 + (B * 64 + 32 * (u // RING + 1))

        def att_stored(b, L):
            return b * 16 + (FREE_A if L.one else 16 * B + FREE_A)

        def norm_no(seg, which):
            first = {"last1": 0, "head2": 2, "loop2": 4, "last2": 2 * B, "end": 2 * B + 1}[seg.name]
            if seg.name == "loop2":
                return seg.it * 3 + (first + which)
            if seg.name in ("last2", "end"):
                return first + (B - 2)
            return first + which

        def dve_tiles(v):
            return SEL_VECTOR[v]

        def slot_read(engine, seg, u):
            if u >= 3 and ("gather", u - 2) not in seg.index:
                engine.wait_ge(x_mm, seg.x0())
            elif u >= 2 or seg.units:
                engine.wait_ge(x_mm, seg.x("gather", u - 2) + 1)

        block = ctx.enter_context(nc.Block())

        @block.sync
        def _(sp):
            def columns(i, name, sem_):
                sp.dma_start(cols[:, i:i + 1], t_in[name]).then_inc(sem_, 16)

            def row(i, name, sem_):
                sp.dma_start(rows[:, i, :], t_in[name]).then_inc(sem_, 16)

            sp.dma_start(xT[:, :], t_in["xT"][0]).then_inc(xT_in, 16)
            for dst, name in ((wqT, "WqT"), (wkT, "WkT"), (wvT, "WvT")):
                sp.dma_start(dst[:, :], t_in[name]).then_inc(w1_in, 16)
            row(0, "bq", w1_in)
            columns(0, "bk", w1_in)
            row(1, "bv", w1_in)
            for dst, name in ((woT, "WoT"), (q2w, "q_wT"), (k2w, "k_wT"), (v2w, "v_wT")):
                sp.dma_start(dst[:, :], t_in[name]).then_inc(w_in, 16)
            for i, name in ((2, "bo"), (3, "v_b")):
                row(i, name, w_in)
            for i, name in ((1, "q_b"), (2, "k_b"), (3, "norm_w"), (4, "norm_b")):
                columns(i, name, w_in)
            sp.sem_inc(att_out, FREE_A)
            sp.wait_ge(w_zero, 2)
            for e in range(SEG):
                m = D >> e
                sp.dma_start(o2w[0:m, e, 0:m], t_in["o_wT"][0:m, 0:m]).then_inc(w_in, 16)
                sp.dma_start(o2b[:, e, 0:m], t_in["o_b"][:, 0:m]).then_inc(w_in, 16)

            def one(dram, b):
                return dram[bass.ds(b, 1)]

            def heads16(dram, b, g):
                return one(dram, b)[:, 16 * g:16 * g + 16].rearrange("b r s t -> (b r s) t")

            def tokens(dram, b):
                return one(dram, b).rearrange("b (a p) d -> (b p) a d", p=P)

            def held(sem_, value):
                sp.wait_ge(sem_, value)
                sp.sem_inc(s_hold, 1)

            def load_unit(L, b, u):
                s, g = L.slot(u), u if L.one else u // 2
                if L.one:
                    sp.dma_start(keys[0:ROWS, s, :], heads16(k1_dram, b, g)).then_inc(kv_in[s], 16)
                    sp.dma_start(values[:, s, :], v1_all[:, g].rearrange("p a b c -> p (a b c)")).then_inc(kv_in[s], 16)
                else:
                    sp.dma_start(keys[0:ROWS, s, :], heads16(k2_dram, b, g)).then_inc(kv_in[s], 16)
                    sp.dma_start(values[:, s, 0:TT * VW], v2_all[:, g].rearrange("p a b -> p (a b)")).then_inc(kv_in[s], 16)
                    sp.dma_start(queries[0:ROWS, s, :], heads16(q2_dram, b, g)).then_inc(kv_in[s], 16)

            def load_positions(b, u):
                sp.dma_start(pos_b[:, u % 2], one(pos_dram, b)[:, 2 * u:2 * u + 2].broadcast_to([HALF, 2, T]))\
                  .then_inc(pb_in[u % 2], 16)

            def guard_rows(seg, u):
                sp.wait_ge(x_read, seg.x("guard", u) + 1)
                L, b, v = seg.unit(u)
                s, q0 = L.slot(v), L.q0(v)
                for g in range(GUARD):
                    sp.dma_start(queries[ROWS + g:ROWS + g + 1, s, q0:q0 + L.nq].rearrange("p (a b) -> p a b", a=QTS),
                                 g_row[QTS * g:QTS * g + QTS, v % RING, 0:L.qw]).then_inc(guard_in[v % RING], 16)

            def units(seg):
                L, b = seg.layer, seg.batch
                for step in UNIT_DMAS.get((seg.name, "start"), ()):
                    step(seg)
                for u in range(L.units):
                    for v in seg.loads(u):
                        held(pv_mm, tile_no(b, L, u, 0) + FREE_P)
                        if v == L.units and seg.prepare:
                            prepared(seg)
                        if v == L.units and seg.between:
                            projected(seg)
                        load_unit(*seg.unit(v))
                    for step in UNIT_DMAS.get((seg.name, u, "early"), ()):
                        step(seg)
                    if seg.has(u + 1):
                        guard_rows(seg, u + 1)
                    if L.one and seg.has(u + 2) and seg.layer_of(u + 2) is L1:
                        held(selt_v, b * 8 + (u + 1))
                        if u + 2 == L.units:
                            held(pos_out, seg.other * 16 + 16)
                        load_positions(*seg.unit(u + 2)[1:])
                    for step in UNIT_DMAS.get((seg.name, u), ()):
                        step(seg)
                if seg.name == "last2":
                    return
                held(x_read, seg.x("scatter" if L.one else "turn", L.units - 1) + 1)
                sp.dma_start(one(att1_dram if L.one else att2_dram, b).rearrange("b p n -> (b p) n"),
                             att[:, :, :].rearrange("p t d -> p (t d)")).then_inc(att_out, 16)

            def load_xT(seg):
                sp.dma_start(xT[:, :], one(t_in["xT"], seg.other).rearrange("b d t -> (b d) t")).then_inc(xT_in, 16)

            def store_k1(seg):
                held(kp_rdy, seg.other + 1)
                for s in range(SLOTS):
                    sp.dma_start(one(k1_dram, seg.other)[:, :, s].rearrange("b d t -> (b d) t"),
                                 k_part[K_SLOTS[s]][:, :]).then_inc(k1_out, 16)

            def store_positions(seg):
                held(pos_rdy, seg.other + 1)
                sp.dma_start(one(pos_dram, seg.other).rearrange("b h t -> (b h) t"), pos_row[0:P:8, :]).then_inc(pos_out, 16)

            def prepared(seg):
                held(k1_out, seg.other * 96 + 96)
                held(y_read, seg.y("v", 1) + 1)

            def load_between(seg):
                held(att_out, att_stored(seg.other, L1) + 16)
                for dst, src in ((x_tok[:, :, :], tokens(t_in["x"], seg.other)),
                                 (att_in[:, :, :].rearrange("p t d -> p (t d)"),
                                  one(att1_dram, seg.other).rearrange("b p n -> (b p) n"))):
                    sp.dma_start(dst, src).then_inc(mid_in, 16)

            def store_x1(seg):
                held(x1_rdy, seg.other + 1)
                sp.dma_start(one(x1_dram, seg.other).rearrange("b p n -> (b p) n"),
                             x1[:, :, :].rearrange("p t d -> p (t d)")).then_inc(x1_out, 16)

            def store_q2(seg):
                held(qp_rdy, seg.other + (B + 1))
                for s in range(SLOTS):
                    sp.dma_start(one(q2_dram, seg.other)[:, :, s].rearrange("b d t -> (b d) t"),
                                 q_part[Q_SLOTS[s]][:, :]).then_inc(qk2_out, 16)

            def store_k2(seg):
                held(kp_rdy, seg.other + (B + 1))
                for s in range(SLOTS):
                    sp.dma_start(one(k2_dram, seg.other)[:, :, s].rearrange("b d t -> (b d) t"),
                                 k_part[K_SLOTS[s]][:, :]).then_inc(qk2_out, 16)

            def projected(seg):
                held(qk2_out, seg.other * 192 + 192)
                held(x1_out, seg.other * 16 + 16)
                held(y_read, seg.y("v2", 1) + 1)

            def load_finish(seg):
                held(att_out, att_stored(seg.done, L2) + 16)
                for dst, src in ((fin_in, att2_dram), (x1_in, x1_dram)):
                    sp.dma_start(dst[:, :, :].rearrange("p t d -> p (t d)"),
                                 one(src, seg.done).rearrange("b p n -> (b p) n")).then_inc(fin_in_s, 16)

            def load_last_x1(seg):
                sp.dma_start(x1_in[:, :, :].rearrange("p t d -> p (t d)"),
                             x1_dram[B - 1]).then_inc(fin_in_s, 16)

            def store_output(seg):
                held(y_rdy, seg.done + 1)
                sp.dma_start(tokens(out, seg.done), y_sb[:, :, :]).then_inc(y_out, 16)

            def output_stored(seg):
                held(y_out, seg.done * 16 + 16)

            UNIT_DMAS = {("loop1", "start"): (load_xT,), ("last1", "start"): (load_between,),
                         ("head2", "start"): (load_between,), ("loop2", "start"): (load_between,),
                         ("loop2", 1): (load_finish,), ("last2", 1): (load_finish,),
                         ("loop1", 3): (store_k1,), ("loop1", 5): (store_positions,),
                         ("last1", 3): (store_x1,), ("last1", 5, "early"): (store_q2, store_k2),
                         ("head2", 5): (store_x1,), ("loop2", 5): (store_x1,),
                         ("head2", 9): (store_q2,), ("loop2", 9): (store_q2, store_output),
                         ("last2", 9): (store_output,),
                         ("head2", 10): (store_k2,), ("loop2", 10): (store_k2,),
                         ("loop2", 13): (output_stored,), ("last2", 13): (output_stored, load_last_x1)}

            def body(seg):
                if seg.name == "first":
                    store_k1(seg)
                    store_positions(seg)
                    prepared(seg)
                    for u in range(3):
                        load_unit(*seg.unit(u))
                    held(pos_out, 16)
                    for u in range(2):
                        load_positions(*seg.unit(u)[1:])
                    guard_rows(seg, 0)
                elif seg.name == "end":
                    store_output(seg)
                else:
                    units(seg)

            run(sp, body)
            sp.wait_ge(y_out, B * 16)
            sp.wait_ge(att_out, (2 * B - 1) * 16 + FREE_A)

        @block.gpsimd
        def _(pool):
            pool.memset(o2w[:, :, :], 0.0).then_inc(w_zero, 1)
            pool.memset(o2b[:, :, :], 0.0).then_inc(w_zero, 1)
            pool.memset(ident[:, :], 0.0).then_inc(c_pool, 1)
            pool.memset(same_head[:, :], 1.0).then_inc(c_pool, 1)
            pool.iota(iota_i[:, :], pattern=[[1, TOP]], base=1, channel_multiplier=0).then_inc(c_pool, 1)
            pool.iota(iota_pi[:, :], pattern=[[HALF, 2]], base=1, channel_multiplier=1).then_inc(c_pool, 1)
            pool.iota(lane[:, :], pattern=[[0, 2]], base=0, channel_multiplier=1).then_inc(c_pool, 1)
            pool.wait_ge(c_pool, 5)
            pool.affine_select(ident[:, :], ident[:, :], [[-1, P]], ALU.not_equal, 1.0, 0, 1).then_inc(c_pool, 1)
            heads = same_head[:, :].rearrange("p (g c) -> p g c", c=8)
            pool.affine_select(heads, heads, [[-8, H1], [0, 8]], ALU.is_ge, 0.0, 0, 1).then_inc(c_pool, 1)
            pool.wait_ge(c_pool, 7)
            pool.affine_select(heads, heads, [[8, H1], [0, 8]], ALU.is_ge, 0.0, 7, -1).then_inc(c_pool, 1)
            pool.memset(v1_all[:, :, :, :, :], 0.0).then_inc(c_pool, 1)
            pool.memset(v2_all[:, :, :, :], 0.0).then_inc(c_pool, 1)
            pool.wait_ge(c_pool, 10)
            pool.memset(v1_all[:, :, :, :, HD1:HD1 + 1], 1.0).then_inc(c_wide, 1)
            pool.memset(v2_all[:, :, :, HD2:HD2 + 1], 1.0).then_inc(c_wide, 1)
            pool.wait_ge(c_rdy, 1)

            def split(no, src, part, rdy):
                n = no * 3
                pool.tensor_tensor(part[0][:, :], src[:, :], ones_t[:, :], ALU.mult).then_inc(p_step, 1)
                pool.wait_ge(p_step, n + 1)
                pool.tensor_tensor(rest[:, :], src[:, :], part[0][:, :], ALU.subtract).then_inc(p_step, 1)
                pool.wait_ge(p_step, n + 2)
                pool.tensor_tensor(part[1][:, :], rest[:, :], ones_t[:, :], ALU.mult).then_inc(p_step, 1)
                pool.wait_ge(p_step, n + 3)
                pool.tensor_tensor(part[2][:, :], rest[:, :], part[1][:, :], ALU.subtract).then_inc(rdy, 1)

            def split_q(seg):
                pool.wait_ge(y_read, seg.y("q", 1) + 1)
                split(seg.other * 2, q32, q_part, qp_rdy)

            def split_k(seg):
                pool.wait_ge(y_read, seg.y("k", 1) + 1)
                pool.wait_ge(qp_rdy, seg.other + 1)
                split(seg.other * 2 + 1, k32, k_part, kp_rdy)

            def split_q2(seg):
                pool.wait_ge(y_read, seg.y("q2", 1) + 1)
                split(seg.other * 2 + (2 * B - (seg.layer is not L1)), q32, q_part, qp_rdy)

            def split_k2(seg):
                pool.wait_ge(y_read, seg.y("k2", 1) + 1)
                pool.wait_ge(qp_rdy, seg.other + (B + 1))
                split(seg.other * 2 + 2 * B, k32, k_part, kp_rdy)

            def sel_tiles(seg, u):
                n, v = seg.units, seg.unit(u)[2]
                if seg.prepare and u >= n:
                    pool.wait_ge(y_read, seg.y("position", 0) + 1)
                slot_read(pool, seg, u)
                pool.sem_inc(p_hold, 1)
                for i in range(dve_tiles(v), 16):
                    h, t = i // TT, i % TT
                    ins = pool.tensor_scalar(sel[:, v % 2, h, t, :], iota_u[:, :], pos_col[:, t, 2 * v + h:2 * v + h + 1],
                                             None, ALU.is_equal)
                ins.then_inc(sel_p, 1)

            def deviations(no):
                pool.wait_ge(sd_rdy, no + 1)
                pool.tensor_tensor(var[:, :], mv[:, :, 1], eps_t[:, :], ALU.add).then_inc(p_var, 1)
                pool.wait_ge(p_var, no + 1)
                pool.tensor_tensor(rstd[:, :], var[:, :], power[:, :], ALU.pow).then_inc(rt_rdy, 1)

            def body(seg):
                if seg.name == "first":
                    split_q(seg)
                    split_k(seg)
                    for u in range(3):
                        sel_tiles(seg, u)
                elif seg.layer is L1:
                    for u in range(L1.units):
                        if seg.prepare and u == 1:
                            split_q(seg)
                        if seg.prepare and u == 2:
                            split_k(seg)
                        if seg.layer_of(u + 3) is L1:
                            sel_tiles(seg, u + 3)
                        if seg.between and u in (1, 2):
                            deviations(norm_no(seg, u - 1))
                    if seg.between:
                        split_q2(seg)
                else:
                    if seg.between:
                        deviations(norm_no(seg, 0))
                        deviations(norm_no(seg, 1))
                    if seg.finish:
                        deviations(norm_no(seg, 2))
                    if seg.between:
                        split_q2(seg)
                        split_k2(seg)

            run(pool, body)

        @block.scalar
        def _(act):
            def exps(seg, u, kt):
                L, n = seg.layer, tile_no(seg.batch, seg.layer, u, kt)
                act.wait_ge(score_mm, n + 1)
                act.wait_ge(pv_mm, n + (1 - RING + FREE_P))
                act.activation(probs[:, kt % RING, 0:L.nq], sbank[kt % 2][:, 0:L.nq], ACT.Exp,
                               scale=L.scale).then_inc(exp_done, 1)

            def copy_queries(seg, u):
                act.wait_ge(x_mm, seg.x("gather", u) + 1)
                v = seg.unit(u)[2]
                act.activation(queries[0:ROWS, v % RING, 0:L1.nq], xbank[0:ROWS, 0:L1.nq], ACT.Copy).then_inc(x_read, 1)

            def copy_maxima(seg, u, q):
                L, b, v = seg.unit(u)
                for c in range(2):
                    n = freed(b, L, v, q, c)
                    act.wait_ge(max_mm, half_no(b, L, v, q, c) + 1)
                    act.wait_ge(copy_red, n + (FREE_C - 2))
                    act.activation(max_sb[0:L.qw, c, :], mbank[(2 * q + c) % M_BANKS][0:L.qw, :], ACT.Copy)\
                       .then_inc(max_cp, 1)

            def copy_values(seg, u):
                L = seg.layer
                act.wait_ge(pv_mm, tile_no(seg.batch, L, u, TT - 1) + (1 + FREE_P))
                act.activation(pv_sb[:, u % 2, 0:L.qw], vbank[:, 0:L.qw], ACT.Copy).then_inc(pv_ev, 1)

            def halves(dst, i):
                return dst[:, 512 * i:512 * i + 512]

            def step(seg, name, i):
                if name == "spread":
                    if i == 0:
                        act.wait_ge(qp_rdy, seg.other + 1)
                    to = q_slots[:, :, :, :].rearrange("p t (g h) (x d s) -> p (t g) h x d s", h=2, x=2, s=SLOTS)
                    frm = q_part[Q_SLOTS[i]][:, :].rearrange("p (a h d) -> p a h d", h=2, d=HD1)
                    for h in range(2):
                        act.activation(to[:, :, h, h, :, i], frm[:, :, h, :], ACT.Copy).then_inc(qs_rdy, 1)
                if name == "upper":
                    act.wait_ge(y_read, seg.y("norm", 1) + 1)
                    act.activation(norms16[:, :], norms[:, :].bitcast(BF16).rearrange("p (t s) -> p t s", s=2)[:, :, 1],
                                   ACT.Copy).then_inc(n16_rdy, 1)
                if name not in ("q", "k", "v", "norm", "at", "xt", "q2", "k2", "v2", "ft"):
                    return
                act.wait_ge(y_mm, seg.y(name, i) + 1)
                if name == "q":
                    ins = act.activation(halves(q32, i), ybank[:, :], ACT.Copy)
                elif name == "k":
                    ins = act.activation(halves(k32, i), ybank[:, :], ACT.Identity, bias=cols[:, 0:1])
                elif name == "v":
                    if seg.layer is None and i == 0:
                        act.wait_ge(c_wide, 4)
                    if seg.layer is not None and i == 0:
                        act.wait_ge(kv_in[3], kv_count(seg.batch, L1, 7))
                        act.wait_ge(kv_in[2], kv_count(seg.batch, L1, 6))
                        act.wait_ge(kv_in[1], kv_count(seg.batch, L1, 5))
                        act.wait_ge(kv_in[0], kv_count(seg.batch, L1, 4))
                    frm = ybank[:, :].rearrange("p (t g h d) -> p g t h d", g=PAIRS, h=2, d=HD1)
                    act.activation(v1_all[:, :, 4 * i:4 * i + 4, 0, 0:HD1], frm[:, :, :, 0, :], ACT.Copy)
                    ins = act.activation(v1_all[:, :, 4 * i:4 * i + 4, 1, 0:HD1], frm[:, :, :, 1, :], ACT.Copy)
                elif name == "norm":
                    ins = act.activation(halves(norms, i), ybank[:, :], ACT.Copy)
                elif name == "at":
                    ins = act.activation(halves(tr, i), ybank[:, :], ACT.Copy)
                elif name == "xt":
                    ins = act.activation(halves(tr, i), ybank[:, :], ACT.Identity, bias=cols[:, 4:5], scale=cols[:, 3:4])
                elif name == "q2":
                    ins = act.activation(halves(q32, i), ybank[:, :], ACT.Identity, bias=cols[:, 1:2])
                elif name == "k2":
                    ins = act.activation(halves(k32, i), ybank[:, :], ACT.Identity, bias=cols[:, 2:3])
                elif name == "v2":
                    if seg.layer is L2 and i == 0:
                        for s in range(RING):
                            act.wait_ge(kv_in[s], kv_count(seg.batch, L2, 8 + 2 * s))
                    ins = act.activation(v2_all[:, :, 4 * i:4 * i + 4, 0:HD2],
                                         ybank[:, :].rearrange("p (t h d) -> p h t d", h=H2, d=HD2), ACT.Copy)
                elif name == "ft":
                    ins = act.activation(halves(fin_tr, i), ybank[:, :], ACT.Copy)
                ins.then_inc(y_read, 1)

            def slot(seg, n):
                for name, i in seg.steps.get(n, ()):
                    step(seg, name, i)

            def body(seg):
                L = seg.layer
                if L is None:
                    for n in sorted(seg.steps):
                        slot(seg, n)
                    if seg.prepare:
                        act.wait_ge(w_in, W_DMAS)
                        for u in range(AHEAD):
                            copy_queries(seg, u)
                        for n in range(2 * QTS - 1):
                            if copied(L1, n % QTS):
                                copy_maxima(seg, n // QTS, n % QTS)
                    return
                for u in range(L.units):
                    for kt in range(TT):
                        exps(seg, u, kt)
                        if L.one and kt == 0 and seg.layer_of(u + 1) is L1:
                            copy_maxima(seg, u + 1, 3)
                        if L.one and kt in (2, 4, 6) and seg.layer_of(u + AHEAD) is L1 and copied(L, kt // 2 - 1):
                            copy_maxima(seg, u + AHEAD, kt // 2 - 1)
                        if kt == 1 and u:
                            copy_values(seg, u - 1)
                        if kt == 0 and ("gather", u + AHEAD) in seg.index:
                            copy_queries(seg, u + AHEAD)
                        for j, at in enumerate(seg.slot_kt):
                            if kt == at:
                                slot(seg, u * seg.slots + j)
                copy_values(seg, L.units - 1)

            act.sem_inc(exp_done, FREE_S)
            act.sem_inc(pv_ev, FREE_V)
            act.sem_inc(copy_red, FREE_C)
            act.wait_ge(c_rdy, 1)
            act.wait_ge(w1_in, 16 * 6)
            run(act, body)

        @block.vector
        def _(dve):
            STEPS = VECTOR_STEPS
            done = [0, 0]

            def own(seg, ins):
                done[1] += 1
                ins.then_inc(v_step, 1)
                dve.wait_ge(v_step, seg.it * STEPS[seg.name] + (done[0] + done[1]))

            dve.memset(ones_row[:, :], 1.0).then_inc(c_vec, 1)
            dve.memset(ones_t[:, :], 1.0).then_inc(c_vec, 1)
            dve.memset(eps_t[:, :], EPS).then_inc(c_vec, 1)
            dve.memset(power[:, :], -0.5).then_inc(c_vec, 1)
            dve.wait_ge(c_pool, 8)
            dve.tensor_copy(ident_b[:, :], ident[:, :]).then_inc(c_vec, 1)
            dve.tensor_copy(iota_u[:, :], iota_i[:, :]).then_inc(c_vec, 1)
            dve.tensor_copy(iota_p[:, :], iota_pi[:, :]).then_inc(c_vec, 1)
            dve.tensor_scalar(lane[:, 1:2], lane[:, 0:1], 7, None, ALU.bitwise_and).then_inc(c_vec, 1)
            dve.wait_ge(c_vec, 8)
            for r in range(ROUNDS - 1):
                dve.tensor_scalar(digit[:, r:r + 1], lane[:, 1:2], SHIFTS[r], None, ALU.logical_shift_left).then_inc(c_vec, 1)
            dve.tensor_scalar(digit[:, ROUNDS - 1:], lane[:, 1:2], 1, None, ALU.min).then_inc(c_vec, 1)
            dve.wait_ge(c_vec, 8 + ROUNDS)
            dve.nop().then_inc(c_rdy, 1)
            dve.memset(keys[ROWS:KR, :, :], 1.0).then_inc(c_wide, 1)
            dve.memset(q_slots[:, :, :, :].rearrange("p a b c -> p (a b c)").bitcast(F32), 0.0).then_inc(c_wide, 1)

            def squares(seg):
                dve.wait_ge(y_read, seg.y("q", 1) + 1)
                own(seg, dve.tensor_tensor(cum[:, :], q32[:, :], q32[:, :], ALU.mult))
                own(seg, dve.tensor_reduce(n2[:, :], cum[:, :].rearrange("p (a d) -> p a d", d=HD1), AX_X, ALU.add))
                dve.tensor_copy(n2rep[:, :, :, :].rearrange("p t h c -> p (t h) c"),
                                n2[:, :].rearrange("p (a o) -> p a o", o=1).broadcast_to([P, TT * H1, 8])).then_inc(n2_rdy, 1)

            def round_start(seg, r):
                if r == 0:
                    dve.wait_ge(n16_rdy, seg.other + 1)
                    own(seg, dve.memset(found[:, 0:1], 0))
                own(seg, dve.tensor_tensor(found[:, 1:2], found[:, 0:1], digit[:, r:r + 1], ALU.bitwise_or))
                upper = SHIFTS[r] >= 16
                reach, frm = (reach16, norms16) if upper else (cmp, norms)
                own(seg, dve.tensor_scalar(reach[:, :], frm[:, :], found[:, 1:2].bitcast(F32), None, ALU.is_ge,
                                           ALU.add, accum_out=count[:, 0:1]))
                dve.tensor_scalar(count_b[:, :], count[:, 0:1], TOP - 0.5, None, ALU.is_ge).then_inc(cnt_rdy, 1)

            def round_finish(seg, r):
                dve.wait_ge(y_mm, seg.y("round", r) + 1)
                last = r == ROUNDS - 1
                dve.tensor_scalar(found[:, 2:3], ybank[:, 0:1], -1.0, 1.0 if last else float(1 << SHIFTS[r]), ALU.add,
                                  ALU.min if last else ALU.mult).then_inc(y_read, 1)
                dve.wait_ge(y_read, seg.y("round", r) + 1)
                own(seg, dve.tensor_tensor(found[:, 0:1], found[:, 0:1], found[:, 2:3], ALU.bitwise_or))

            def positions(seg, part):
                limit = found[:, 0:1].bitcast(F32)
                if part == 0:
                    own(seg, dve.tensor_scalar(cmp[:, :], norms[:, :], limit, None, ALU.is_gt, ALU.add,
                                               accum_out=count[:, 0:1]))
                    own(seg, dve.tensor_scalar(count[:, 1:2], count[:, 0:1], -1.0, float(TOP), ALU.mult, ALU.add))
                    own(seg, dve.tensor_scalar(norms[:, :], norms[:, :], limit, None, ALU.is_equal))
                elif part == 1:
                    own(seg, dve.tensor_tensor_scan(cum[:, :], ones_t[:, :], norms[:, :], 0.0, ALU.mult, ALU.add))
                    own(seg, dve.scalar_tensor_tensor(norms[:, :], cum[:, :], count[:, 1:2], norms[:, :],
                                                      ALU.is_le, ALU.mult))
                elif part == 2:
                    own(seg, dve.tensor_tensor(cmp[:, :], cmp[:, :], norms[:, :], ALU.add))
                    own(seg, dve.tensor_tensor_scan(cum[:, :], ones_t[:, :], cmp[:, :], 0.0, ALU.mult, ALU.add))
                else:
                    dve.tensor_tensor(pos_row[:, :], cum[:, :], cmp[:, :], ALU.mult).then_inc(pos_rdy, 1)

            def position_columns(seg):
                dve.wait_ge(y_mm, seg.y("position", 0) + 1)
                if seg.layer is not None:
                    dve.wait_ge(sel_p, seg.batch * 8 + 8)
                dve.tensor_copy(pos_col[:, :, :], ybank_b.rearrange("p (t h c) -> p t h c", t=TT, c=8)[:, :, :, 0])\
                   .then_inc(y_read, 1)
                dve.wait_ge(y_read, seg.y("position", 0) + 1)

            def build_sel(seg, u):
                v = seg.unit(u)[2]
                slot_read(dve, seg, u)
                for i in range(dve_tiles(v)):
                    h, t = i // TT, i % TT
                    ins = dve.tensor_scalar(sel[:, v % 2, h, t, :], iota_u[:, :], pos_col[:, t, 2 * v + h:2 * v + h + 1],
                                            None, ALU.is_equal)
                ins.then_inc(sel_v, 1)

            def build_sel_t(seg, u):
                dve.wait_ge(pb_in[u % 2], seg.batch * 64 + 16 * (u // 2 + 1))
                for h in range(2):
                    for half in range(2):
                        ins = dve.tensor_scalar(sel_t[:, u % 2, h, half, :], pos_b[:, u % 2, h, :],
                                                iota_p[0:HALF, half:half + 1], None, ALU.is_equal)
                ins.then_inc(selt_v, 1)

            def maximum(seg, u, q):
                L, b, v = seg.unit(u)
                for c in range(2):
                    to = mx2[0:L.qw, v % 2, q, c:c + 1]
                    if copied(L, q):
                        dve.wait_ge(max_cp, freed(b, L, v, q, c))
                        dve.tensor_scalar(max_sb[0:L.qw, c, :], max_sb[0:L.qw, c, :], 1.0, None, ALU.mult, ALU.max,
                                          accum_out=to).then_inc(copy_red, 1)
                    else:
                        dve.wait_ge(max_mm, half_no(b, L, v, q, c) + 1)
                        dve.tensor_reduce(to, mbank[(2 * q + c) % M_BANKS][0:L.qw, :], AX_X, ALU.max).then_inc(max_red, 1)

            def guard_parts(seg, u):
                L, b, v = seg.unit(u)
                w = L.qw
                if L.one:
                    dve.wait_ge(max_red, freed(b, L, v, max(set(range(QTS)) - set(COPIED)), 1))
                    dve.wait_ge(copy_red, freed(b, L, v, COPIED[-1], 1) + FREE_C)
                else:
                    dve.wait_ge(max_red, freed(b, L, v, QTS - 1, 1))
                g, m = g_part[0:w, v % 2], mx[0:w, :]
                own(seg, dve.tensor_reduce(m, mx2[0:w, v % 2], AX_X, ALU.max))
                own(seg, dve.tensor_scalar(g[:, 0, :], m, -1.0, None, ALU.mult))
                dve.scalar_tensor_tensor(g[:, 1, :], m, -1.0, g[:, 0, :], ALU.mult, ALU.subtract).then_inc(gp_rdy, 1)

            def guard_copy(seg, u):
                L, b, v = seg.unit(u)
                dve.wait_ge(x_mm, seg.x("guard", u) + 1)
                dve.tensor_copy(g_row[:, v % RING, 0:L.qw], xbank_b[0:GUARD * QTS, 0:L.qw]).then_inc(x_read, 1)

            def norm_outputs(seg, u):
                L, w, d = seg.layer, seg.layer.qw, seg.layer.hd
                x = seg.x("turn", u) + 1
                dve.wait_ge(x_mm, x)
                turned = xbank[0:w, 0:P].rearrange("p (g r) -> p g r", r=VW)
                own(seg, dve.reciprocal(den[0:w, :], turned[:, :, d]))
                share = den[0:w, :].rearrange("p (g o) -> p g o", o=1).broadcast_to([w, QTS, d])
                if not L.one:
                    t0, c0 = QTS * (u % 2), HD2 * (u // 2)
                    if u == 0:
                        dve.wait_ge(att_out, att_stored(seg.batch, L2))
                    dve.tensor_tensor(att[:, t0:t0 + QTS, c0:c0 + HD2], turned[:, :, 0:d], share, ALU.mult).then_inc(x_read, 1)
                    return
                dve.tensor_tensor(o_sel[:, :, :], turned[:, :, 0:d], share, ALU.mult).then_inc(x_read, 1)
                dve.wait_ge(x_read, x)
                parts = o_part[:, u % 2]
                own(seg, dve.tensor_copy(parts[:, :, 0, :], o_sel[:, :, :]))
                dve.tensor_tensor(o_rest[:, :, :], o_sel[:, :, :], parts[:, :, 0, :], ALU.subtract)
                own(seg, dve.tensor_tensor(parts[:, :, 1, :], o_sel[:, :, :], parts[:, :, 0, :], ALU.subtract))
                dve.tensor_tensor(parts[:, :, 2, :], o_rest[:, :, :], parts[:, :, 1, :], ALU.subtract).then_inc(on_rdy, 1)

            def sum_scattered(seg, u):
                dve.wait_ge(x_mm, seg.x("scatter", u) + 1)
                if u == 0:
                    dve.wait_ge(att_out, att_stored(seg.batch, L1))
                x = xbank[:, 0:TT * 2 * 3 * HD1].rearrange("p (t h s d) -> p t h d s", t=TT, h=2, s=3)
                dve.tensor_reduce(att[:, :, 16 * u:16 * u + 8], x[:, :, 0], AX_X, ALU.add)
                dve.tensor_reduce(att[:, :, 16 * u + 8:16 * u + 16], x[:, :, 1], AX_X, ALU.add).then_inc(x_read, 1)

            def statistics(seg, src):
                for t in range(TT):
                    ins = dve.bn_stats(stats[:, t, :], src[:, t, :])
                own(seg, ins)
                dve.sem_inc(v_hold, 1)
                for t in range(TT):
                    ins = dve.bn_aggr(mv[:, t, :], stats[:, t, :])
                ins.then_inc(sd_rdy, 1)

            def normalise(no, src, dst, rdy):
                dve.wait_ge(rt_rdy, no + 1)
                for t in range(TT):
                    ins = dve.tensor_scalar(dst[:, t, :], src[:, t, :], mv[:, t, 0:1], rstd[:, t:t + 1],
                                            ALU.subtract, ALU.mult)
                ins.then_inc(rdy, 1)

            def split_k2(seg):
                dve.wait_ge(y_read, seg.y("k2", 1) + 1)
                own(seg, dve.tensor_copy(k_part[0][:, :], k32[:, :]))
                own(seg, dve.tensor_tensor(norms[:, :], k32[:, :], k_part[0][:, :], ALU.subtract))
                own(seg, dve.tensor_copy(k_part[1][:, :], norms[:, :]))
                dve.tensor_tensor(k_part[2][:, :], norms[:, :], k_part[1][:, :], ALU.subtract).then_inc(kp_rdy, 1)

            def start(seg, name, i):
                if name == "squares":
                    squares(seg)
                elif name == "positions":
                    positions(seg, i)
                elif name == "split_k2":
                    split_k2(seg)
                elif name == "norm1":
                    statistics(seg, zt)
                elif name == "norm2":
                    normalise(norm_no(seg, 0), zt, x1, x1_rdy)
                elif name == "stats2":
                    dve.wait_ge(x1_rdy, seg.other + 1)
                    statistics(seg, x1)
                elif name == "norm3":
                    normalise(norm_no(seg, 1), x1, xh, xh_rdy)
                elif name == "norm4":
                    statistics(seg, fin_in)
                elif name == "norm5":
                    normalise(norm_no(seg, 2), fin_in, y_sb, y_rdy)

            def finish(seg, name, i):
                t0 = 4 * i
                if name == "norm" and i == 1:
                    round_start(seg, 0)
                elif name == "round":
                    round_finish(seg, i)
                    if i + 1 < ROUNDS:
                        round_start(seg, i + 1)
                elif name == "position":
                    position_columns(seg)
                elif name == "y":
                    dve.wait_ge(mid_in, seg.other * 32 + 32)
                    dve.wait_ge(y_mm, seg.y("y", i) + 1)
                    dve.tensor_tensor(zt[:, t0:t0 + 4, :].rearrange("p t d -> p (t d)"), ybank[:, :],
                                      x_tok[:, t0:t0 + 4, :].rearrange("p t d -> p (t d)"), ALU.add).then_inc(y_read, 1)
                    dve.wait_ge(y_read, seg.y("y", i) + 1)
                elif name == "fo":
                    dve.wait_ge(fin_in_s, finish_loads(seg))
                    dve.wait_ge(y_mm, seg.y("fo", i) + 1)
                    dve.scalar_tensor_tensor(fin_in[:, t0:t0 + 4, :].rearrange("p t d -> p (t d)"),
                                             x1_in[:, t0:t0 + 4, :].rearrange("p t d -> p (t d)"), 2.0, ybank[:, :],
                                             ALU.mult, ALU.add).then_inc(y_read, 1)
                    dve.wait_ge(y_read, seg.y("fo", i) + 1)

            def slot(seg, n, between=()):
                for name, i in seg.steps.get(n, ()):
                    start(seg, name, i)
                for work in between:
                    work()
                for name, i in seg.steps.get(n, ()):
                    finish(seg, name, i)

            def first_units(seg):
                for n in sorted(seg.steps):
                    slot(seg, n)
                for u in range(3):
                    build_sel(seg, u)
                for q in range(QTS):
                    maximum(seg, 0, q)
                guard_parts(seg, 0)
                guard_copy(seg, 0)
                for q in range(QTS - 1):
                    maximum(seg, 1, q)

            def first_layer(seg):
                n = L1.units
                for u in range(n):
                    if seg.layer_of(u + 1) is L1:
                        maximum(seg, u + 1, QTS - 1)
                    guard_parts(seg, u + 1)
                    after = seg.prepare and u + 3 == n
                    build = [lambda: build_sel(seg, u + 3)] if seg.layer_of(u + 3) is L1 else []
                    slot(seg, u * 4, [] if after else build)
                    maximum(seg, u + AHEAD, 0)
                    if u > 0:
                        norm_outputs(seg, u - 1)
                    guard_copy(seg, u + 1)
                    slot(seg, u * 4 + 1, [lambda: build_sel_t(seg, u)])
                    maximum(seg, u + AHEAD, 1)
                    if u > 0:
                        sum_scattered(seg, u - 1)
                    slot(seg, u * 4 + 2)
                    maximum(seg, u + AHEAD, 2)
                    last = [lambda: maximum(seg, u + AHEAD, 3)] if seg.layer_of(u + AHEAD) is L2 else []
                    slot(seg, u * 4 + 3, (build if after else []) + last)
                norm_outputs(seg, n - 1)
                sum_scattered(seg, n - 1)

            def second_layer(seg):
                n = L2.units
                for u in range(n):
                    ahead = seg.has(u + AHEAD)
                    if seg.has(u + 1):
                        guard_parts(seg, u + 1)
                    if ahead:
                        maximum(seg, u + AHEAD, 0)
                    slot(seg, 2 * u)
                    if seg.has(u + 1):
                        guard_copy(seg, u + 1)
                    if ahead:
                        maximum(seg, u + AHEAD, 1)
                    if u > 0:
                        norm_outputs(seg, u - 1)
                    if ahead:
                        maximum(seg, u + AHEAD, 2)
                    slot(seg, 2 * u + 1, [lambda: maximum(seg, u + AHEAD, 3)] if ahead else [])
                norm_outputs(seg, n - 1)

            def body(seg):
                if seg.layer is L1:
                    first_layer(seg)
                elif seg.layer is L2:
                    second_layer(seg)
                elif seg.prepare:
                    first_units(seg)
                else:
                    for n in sorted(seg.steps):
                        slot(seg, n)
                assert done[1] == STEPS[seg.name], (seg.name, done[1])
                done[0] += done[1] * seg.times
                done[1] = 0

            run(dve, body)

        @block.tensor
        def _(pe):
            def with_row(dst, lhsT, rhs, bias):
                pe.matmul(dst, lhsT, rhs, start=True, stop=False)
                return pe.matmul(dst, ones_row[:, :], bias, start=False, stop=True)

            def tile(bank, t, w=P):
                return bank[:, t * w:t * w + w]

            def unit_bank(seg, *key):
                if seg.before_x + seg.index[key]:
                    pe.wait_ge(x_read, seg.x(*key))

            def step_bank(seg, *key):
                if seg.before_y + seg.step_index[key]:
                    pe.wait_ge(y_read, seg.y(*key))

            def gather(seg, u):
                unit_bank(seg, "gather", u)
                _, b, v = seg.unit(u)
                if v == 0:
                    pe.wait_ge(qs_rdy, b * 12 + 12)
                pe.wait_ge(sel_v, b * 8 + (v + 1))
                pe.wait_ge(sel_p, b * 8 + (v + 1))
                for h in range(2):
                    for t in range(TT):
                        ins = pe.matmul(xbank[0:ROWS, h * TOP:h * TOP + TOP], q_slots[:, t, 2 * v + h, :],
                                        sel[:, v % 2, h, t, :], start=(t == 0), stop=(t == TT - 1))
                ins.then_inc(x_mm, 1)

            def bank_emptied(seg, L, b, v, h):
                if h >= M_BANKS:
                    h -= M_BANKS
                elif v or seg.units:
                    if v == 0 and seg.name == "last1":
                        L, b, v = L1, B, 0
                    v, h = v - 1, (6, 7, 5)[h]
                else:
                    return
                q, c = h // 2, h % 2
                pe.wait_ge(max_cp if copied(L, q) else max_red, freed(b, L, v, q, c))

            def max_scores(seg, u, q, halves=(0, 1)):
                L, b, v = seg.unit(u)
                s = L.slot(v)
                if q == 0 and 0 in halves:
                    pe.wait_ge(kv_in[s], kv_count(b, L, v))
                    if L.one:
                        pe.wait_ge(x_read, seg.x("gather", u) + 1)
                c0 = L.q0(v) + q * L.qw
                for c in halves:
                    bank_emptied(seg, L, b, v, 2 * q + c)
                    pe.matmul(mbank[(2 * q + c) % M_BANKS][0:L.qw, :], queries[0:ROWS, s, c0:c0 + L.qw],
                              keys[0:ROWS, s, c * 512:c * 512 + 512], start=True, stop=True).then_inc(max_mm, 1)

            def turn_guard(seg, u):
                L, b, v = seg.unit(u)
                w = L.qw
                unit_bank(seg, "guard", u)
                pe.wait_ge(gp_rdy, unit_no(b, L, v) + 1)
                pe.transpose(xbank_b[0:GUARD * QTS, 0:w], g_part[0:w, v % 2].rearrange("p a b -> p (a b)"),
                             ident_b[0:w, 0:w]).then_inc(x_mm, 1)

            def scores(seg, u, kt):
                L, b = seg.layer, seg.batch
                s, q0 = L.slot(u), L.q0(u)
                if kt == 0:
                    pe.wait_ge(guard_in[u % RING], guard_count(b, L, u))
                pe.wait_ge(exp_done, tile_no(b, L, u, kt) + (1 - 2 + FREE_S))
                pe.matmul(sbank[kt % 2][:, 0:L.nq], keys[:, s, kt * P:kt * P + P],
                          queries[:, s, q0:q0 + L.nq], start=True, stop=True).then_inc(score_mm, 1)

            def add_values(seg, u, kt):
                L, b = seg.layer, seg.batch
                pe.wait_ge(exp_done, tile_no(b, L, u, kt) + (1 + FREE_S))
                if kt == 0:
                    pe.wait_ge(pv_ev, unit_no(b, L, u) + FREE_V)
                s, w = L.slot(u), L.qw
                for g in range(QTS):
                    c = (kt * 2 + g // 2) * VW if L.one else kt * VW
                    ins = pe.matmul(vbank[VW * g:VW * g + VW, 0:w], values[:, s, c:c + VW],
                                    probs[:, kt % RING, g * w:g * w + w], start=(kt == 0), stop=(kt == TT - 1))
                ins.then_inc(pv_mm, 1)

            def values_behind(seg, u, kt):
                if u or kt >= 2:
                    add_values(seg, u if kt >= 2 else u - 1, (kt - 2) % TT)

            def turn_outputs(seg, u):
                L, w = seg.layer, seg.layer.qw
                unit_bank(seg, "turn", u)
                pe.wait_ge(pv_ev, unit_no(seg.batch, L, u) + (1 + FREE_V))
                pe.transpose(xbank[0:w, 0:P], pv_sb[:, u % 2, 0:w], ident[:, :]).then_inc(x_mm, 1)

            def scatter(seg, u):
                unit_bank(seg, "scatter", u)
                pe.wait_ge(on_rdy, seg.batch * 8 + (u + 1))
                pe.wait_ge(selt_v, seg.batch * 8 + (u + 1))
                for t in range(TT):
                    for h in range(2):
                        c = (t * 2 + h) * 3 * HD1
                        for half in range(2):
                            ins = pe.matmul(xbank[:, c:c + 3 * HD1], sel_t[:, u % 2, h, half, t * P:t * P + P],
                                            o_part[:, u % 2, 2 * h + half].rearrange("p s d -> p (s d)"),
                                            start=(half == 0), stop=(half == 1))
                ins.then_inc(x_mm, 1)

            def step(seg, name, i):
                if name not in BANK_STEPS:
                    return
                step_bank(seg, name, i)
                four = range(4 * i, 4 * i + 4)
                if name == "q":
                    if i == 0:
                        pe.wait_ge(xT_in, seg.other * 16 + 16)
                    for t in four:
                        ins = with_row(tile(ybank, t % 4), tile(xT, t), wqT[:, :], rows[:, 0, :])
                elif name == "k":
                    ins = pe.matmul(ybank[:, :], wkT[:, :], tile(xT, i, 512), start=True, stop=True)
                elif name == "v":
                    for t in four:
                        ins = with_row(tile(ybank, t % 4), tile(xT, t), wvT[:, :], rows[:, 1, :])
                elif name == "norm":
                    pe.wait_ge(n2_rdy, seg.other + 1)
                    for t in four:
                        ins = pe.transpose(tile(ybank, t % 4), n2rep[:, t].rearrange("p h c -> p (h c)"), ident[:, :])
                elif name == "round":
                    pe.wait_ge(cnt_rdy, seg.other * ROUNDS + (i + 1))
                    ins = pe.matmul(ybank[:, 0:1], same_head[:, :], count_b[:, :], start=True, stop=True)
                elif name == "position":
                    pe.wait_ge(pos_rdy, seg.other + 1)
                    for t in range(TT):
                        ins = pe.transpose(tile(ybank_b, t), tile(pos_row, t), ident_b[:, :])
                elif name == "at":
                    if i == 0:
                        pe.wait_ge(mid_in, seg.other * 32 + 32)
                    for t in four:
                        ins = pe.transpose(tile(ybank, t % 4), att_in[:, t, :], ident[:, :])
                elif name == "y":
                    for t in four:
                        ins = with_row(tile(ybank, t % 4), tile(tr, t), woT[:, :], rows[:, 2, :])
                elif name == "xt":
                    pe.wait_ge(xh_rdy, seg.other + 1)
                    for t in four:
                        ins = pe.transpose(tile(ybank, t % 4), xh[:, t, :], ident[:, :])
                elif name in ("q2", "k2"):
                    w = q2w if name == "q2" else k2w
                    for e in (2 * i, 2 * i + 1):
                        m, c = D >> e, T // SEG
                        ins = pe.matmul(tile(ybank, e % 2, c), w[0:m, :], tr[0:m, e * c:e * c + c], start=True, stop=True)
                elif name == "v2":
                    for t in four:
                        m = D >> (t * SEG // TT)
                        ins = with_row(tile(ybank, t % 4), tr[0:m, t * P:t * P + P], v2w[0:m, :], rows[:, 3, :])
                elif name == "ft":
                    if i == 0 and seg.name == "end":
                        pe.wait_ge(x_read, seg.x0())
                    elif i == 0:
                        pe.wait_ge(fin_in_s, finish_loads(seg))
                    frm = att if seg.name == "end" else fin_in
                    for t in four:
                        ins = pe.transpose(tile(ybank, t % 4), frm[:, t, :], ident[:, :])
                elif name == "fo":
                    for t in four:
                        e = t * SEG // TT
                        m = D >> e
                        ins = with_row(tile(ybank, t % 4), fin_tr[0:m, t * P:t * P + P], o2w[0:m, e, :], o2b[:, e, :])
                ins.then_inc(y_mm, 1)

            def slot(seg, n):
                for name, i in seg.steps.get(n, ()):
                    step(seg, name, i)

            def first_units(seg):
                pe.wait_ge(w_in, W_DMAS)
                for u in range(AHEAD):
                    gather(seg, u)
                for q in range(QTS):
                    max_scores(seg, 0, q)
                turn_guard(seg, 0)
                for q in range(QTS - 1):
                    max_scores(seg, 1, q)

            def first_layer(seg):
                n = L1.units
                for u in range(n):
                    for kt in range(TT):
                        scores(seg, u, kt)
                        values_behind(seg, u, kt)
                        if kt == 0 and seg.layer_of(u + 1) is L1:
                            max_scores(seg, u + 1, QTS - 1)
                        if kt == 0 and ("gather", u + AHEAD) in seg.index:
                            gather(seg, u + AHEAD)
                        if kt in (2, 4, 6):
                            max_scores(seg, u + AHEAD, kt // 2 - 1)
                        if kt == 7 and seg.layer_of(u + AHEAD) is L2:
                            max_scores(seg, u + AHEAD, 3)
                        if kt == 3 and u:
                            turn_outputs(seg, u - 1)
                        if kt == 4:
                            turn_guard(seg, u + 1)
                        if kt == 5 and u:
                            scatter(seg, u - 1)
                        for j, at in enumerate(seg.slot_kt):
                            if kt == at:
                                slot(seg, u * seg.slots + j)
                values_behind(seg, n, 0)
                values_behind(seg, n, 1)
                turn_outputs(seg, n - 1)
                scatter(seg, n - 1)

            def second_layer(seg):
                n = L2.units
                for u in range(n):
                    for kt in range(TT):
                        scores(seg, u, kt)
                        values_behind(seg, u, kt)
                        if seg.has(u + AHEAD):
                            max_scores(seg, u + AHEAD, kt // 2, (kt % 2,))
                        if kt == 3 and seg.has(u + 1):
                            turn_guard(seg, u + 1)
                        if kt == 4 and u:
                            turn_outputs(seg, u - 1)
                        for j, at in enumerate(seg.slot_kt):
                            if kt == at:
                                slot(seg, u * seg.slots + j)
                values_behind(seg, n, 0)
                values_behind(seg, n, 1)
                turn_outputs(seg, n - 1)

            def body(seg):
                if seg.layer is L1:
                    first_layer(seg)
                elif seg.layer is L2:
                    second_layer(seg)
                else:
                    for n in sorted(seg.steps):
                        slot(seg, n)
                    if seg.prepare:
                        first_units(seg)

            pe.sem_inc(pv_mm, FREE_P)
            pe.wait_ge(c_rdy, 1)
            pe.wait_ge(w1_in, 16 * 6)
            run(pe, body)


_TURNED = {"WqT": "L0_attn_Wq", "WkT": "L0_attn_Wk", "WvT": "L0_attn_Wv", "WoT": "L0_attn_Wo",
           "q_wT": "L0_ffn_q_w", "k_wT": "L0_ffn_k_w", "v_wT": "L0_ffn_v_w", "o_wT": "L0_ffn_o_w"}
_ROWS = {"bq": "L0_attn_bq", "bv": "L0_attn_bv", "bo": "L0_attn_bo", "v_b": "L0_ffn_v_b", "o_b": "L0_ffn_o_b"}
_COLS = {"bk": "L0_attn_bk", "q_b": "L0_ffn_q_b", "k_b": "L0_ffn_k_b", "norm_w": "L0_ffn_norm_w",
         "norm_b": "L0_ffn_norm_b"}


def kernel(**inputs):
    import numpy as _np
    import concourse.bacc as _bacc
    from concourse.bass_utils import run_bass_kernel_spmd as _run

    nc = _bacc.Bacc("TRN2", target_bir_lowering=False, num_devices=1)
    x = _np.asarray(inputs["L0_attn_x"])
    given = {"x": x, "xT": x.transpose(0, 2, 1)}
    given |= {k: _np.asarray(inputs[n]).T for k, n in _TURNED.items()}
    given |= {k: _np.asarray(inputs[n]).reshape(1, D) for k, n in _ROWS.items()}
    given |= {k: _np.asarray(inputs[n]).reshape(D, 1) for k, n in _COLS.items()}
    arrays, t_in = {}, {}
    for name, a in given.items():
        a = _np.ascontiguousarray(a)
        arrays[f"in_{name}"] = a
        t_in[name] = nc.dram_tensor(f"in_{name}", a.shape, F32, kind="ExternalInput").ap()
    out = nc.dram_tensor("out", (B, T, D), F32, kind="ExternalOutput").ap()
    build(nc, t_in, out)
    r = _run(nc, [arrays], core_ids=[0])
    return r.results[0]["out"]
```
